# Optimizing a Trainium2 kernel written in Bass

```python
import numpy as np
import jax
import jax.numpy as jnp

def _softmax(x, axis=-1):
    return jax.nn.softmax(x, axis=axis)

def _gelu(x):
    return jax.nn.gelu(x, approximate=True)

def _silu(x):
    return jax.nn.silu(x)

def _sigmoid(x):
    return jax.nn.sigmoid(x)

def _layernorm(x, axis=-1, eps=1e-05):
    m = jnp.mean(x, axis=axis, keepdims=True)
    v = jnp.var(x, axis=axis, keepdims=True)
    return (x - m) / jnp.sqrt(v + eps)

def _scatter_add(tgt, idx, src, axis=0):
    return tgt.at[idx].add(src)

def _segment_sum(src, seg, n):
    return jax.ops.segment_sum(src, seg, n)
kernel_name = 'mk_seq_preln_d1_jaxref_r8_e69fda'

def setup_inputs(seed: int=0):
    np.random.seed(seed)
    _w = jnp.asarray

    def _L0_attn_setup():
        import jax, jax.numpy as jnp
        import numpy as np
        B, S, D_IN, D_OUT = (4, 256, 256, 256)
        key = jax.random.key(seed)
        k1, k2, k3, k4 = jax.random.split(key, 4)
        x = jax.random.normal(k1, (B, S, D_IN), dtype=jnp.float32)
        scale = 1.0 / np.sqrt(D_IN)
        Wq = jax.random.normal(k2, (D_IN, D_OUT), dtype=jnp.float32) * scale
        Wk = jax.random.normal(k3, (D_IN, D_OUT), dtype=jnp.float32) * scale
        Wv = jax.random.normal(k4, (D_IN, D_OUT), dtype=jnp.float32) * scale
        return {'x': x, 'Wq': Wq, 'Wk': Wk, 'Wv': Wv}
    _L0_attn_in = _L0_attn_setup()

    def _L0_ffn_setup():
        import jax, jax.numpy as jnp
        import numpy as np
        B, S, H = (4, 128, 256)
        E = 16
        K = 2
        I = 128
        N_SHARED = 2
        I_SHARED = I * N_SHARED
        RATIO = 0.1
        EPS = 1e-09

        def _swiglu(x, wg, wu, wd):
            return jax.nn.silu(x @ wg) * (x @ wu) @ wd
        key = jax.random.key(seed)
        ks = jax.random.split(key, 9)
        scale = 0.02
        x = jax.random.normal(ks[0], (B, S, H), dtype=jnp.float32)
        centroids = jax.random.normal(ks[1], (E, H), dtype=jnp.float32)
        gate_bias = jnp.zeros((E,), dtype=jnp.float32)
        wg_s = jax.random.normal(ks[2], (H, I_SHARED), dtype=jnp.float32) * scale
        wu_s = jax.random.normal(ks[3], (H, I_SHARED), dtype=jnp.float32) * scale
        wd_s = jax.random.normal(ks[4], (I_SHARED, H), dtype=jnp.float32) * scale
        wg = jax.random.normal(ks[5], (E, H, I), dtype=jnp.float32) * scale
        wu = jax.random.normal(ks[6], (E, H, I), dtype=jnp.float32) * scale
        wd = jax.random.normal(ks[7], (E, I, H), dtype=jnp.float32) * scale
        return {'x': x, 'centroids': centroids, 'gate_bias': gate_bias, 'wg_s': wg_s, 'wu_s': wu_s, 'wd_s': wd_s, 'wg': wg, 'wu': wu, 'wd': wd}
    _L0_ffn_in = _L0_ffn_setup()
    _d = {'L0_attn_x': _L0_attn_in['x'], 'L0_attn_Wq': _L0_attn_in['Wq'], 'L0_attn_Wk': _L0_attn_in['Wk'], 'L0_attn_Wv': _L0_attn_in['Wv'], 'L0_ffn_centroids': _L0_ffn_in['centroids'], 'L0_ffn_gate_bias': _L0_ffn_in['gate_bias'], 'L0_ffn_wg_s': _L0_ffn_in['wg_s'], 'L0_ffn_wu_s': _L0_ffn_in['wu_s'], 'L0_ffn_wd_s': _L0_ffn_in['wd_s'], 'L0_ffn_wg': _L0_ffn_in['wg'], 'L0_ffn_wu': _L0_ffn_in['wu'], 'L0_ffn_wd': _L0_ffn_in['wd']}
    _x0 = _d['L0_attn_x']
    _d['L0_attn_x'] = jax.random.normal(jax.random.fold_in(jax.random.key(seed), 1), (4, 512, 256), dtype=_x0.dtype)
    del _x0
    return _d

def reference(L0_attn_x, L0_attn_Wq, L0_attn_Wk, L0_attn_Wv, L0_ffn_centroids, L0_ffn_gate_bias, L0_ffn_wg_s, L0_ffn_wu_s, L0_ffn_wd_s, L0_ffn_wg, L0_ffn_wu, L0_ffn_wd):

    def _L0_attn_ref(x, Wq, Wk, Wv):
        import jax, jax.numpy as jnp
        import numpy as np
        B, S, D_IN, D_OUT = (4, 256, 256, 256)
        q = x @ Wq
        k = x @ Wk
        v = x @ Wv
        d_out = q.shape[-1]
        inv_sqrt_d = jnp.asarray(1.0 / np.sqrt(d_out), dtype=x.dtype)
        scores = jnp.einsum('bqd,bkd->bqk', q, k) * inv_sqrt_d
        n = scores.shape[-1]
        causal = jnp.tril(jnp.ones((n, n), dtype=bool))
        scores = jnp.where(causal[None, :, :], scores, jnp.asarray(-jnp.inf, scores.dtype))
        attn = jax.nn.softmax(scores, axis=-1)
        return jnp.einsum('bqk,bkd->bqd', attn, v)

    def _L0_ffn_ref(x, centroids, gate_bias, wg_s, wu_s, wd_s, wg, wu, wd):
        import jax, jax.numpy as jnp
        import numpy as np
        B, S, H = (4, 128, 256)
        E = 16
        K = 2
        I = 128
        N_SHARED = 2
        I_SHARED = I * N_SHARED
        RATIO = 0.1
        EPS = 1e-09

        def _swiglu(x, wg, wu, wd):
            return jax.nn.silu(x @ wg) * (x @ wu) @ wd
        shared = _swiglu(x, wg_s, wu_s, wd_s) * RATIO
        affinity = jax.nn.sigmoid(jnp.einsum('bsh,eh->bse', x, centroids))
        biased = affinity + gate_bias
        _, top_idx = jax.lax.top_k(biased, K)
        top_aff = jnp.take_along_axis(affinity, top_idx, axis=-1)
        weights = top_aff / (top_aff.sum(-1, keepdims=True) + EPS)
        mask = (jax.nn.one_hot(top_idx, E, dtype=x.dtype) * weights[..., None]).sum(-2)
        routed = jnp.zeros_like(x)
        for e in range(E):
            routed = routed + mask[..., e:e + 1] * _swiglu(x, wg[e], wu[e], wd[e])
        return shared + routed
    x = L0_attn_x
    x = x + _L0_attn_ref(_layernorm(x, axis=-1), L0_attn_Wq, L0_attn_Wk, L0_attn_Wv)
    x = x + _L0_ffn_ref(_layernorm(x, axis=-1), L0_ffn_centroids, L0_ffn_gate_bias, L0_ffn_wg_s, L0_ffn_wu_s, L0_ffn_wd_s, L0_ffn_wg, L0_ffn_wu, L0_ffn_wd)
    return x

_drawn_inputs = setup_inputs


def setup_inputs(seed=0):
    import zlib

    import numpy as np

    out = dict(_drawn_inputs(seed))
    spreads = {'L0_ffn_gate_bias': (0.0, 0.8)}
    factors = {'L0_ffn_centroids': 8.0,
     'L0_ffn_wg_s': 8.0,
     'L0_ffn_wu_s': 8.0,
     'L0_ffn_wd_s': 8.0,
     'L0_ffn_wg': 6.837,
     'L0_ffn_wu': 6.769,
     'L0_ffn_wd': 6.769}
    for name, (base, spread) in spreads.items():
        noise = np.random.default_rng([zlib.crc32(name.encode()), seed]).standard_normal(out[name].shape)
        drawn = base * np.exp(spread * noise) if base else spread * noise
        out[name] = jnp.asarray(drawn.astype(out[name].dtype))
    for name, factor in factors.items():
        out[name] = (out[name] * factor).astype(out[name].dtype)
    return out
```

```python
from contextlib import ExitStack

import concourse.bass as bass
from concourse import mybir

P = 128
ALU = mybir.AluOpType
ACT = mybir.ActivationFunctionType
AX = mybir.AxisListType.X
F32 = mybir.dt.float32
F32R = mybir.dt.float32r
BF16 = mybir.dt.bfloat16
U32 = mybir.dt.uint32
I32 = mybir.dt.int32

LEAST_LOGIT = -87.0
LN_EPS = 1e-5
GATE_EPS = 1e-9
SHARED_RATIO = 0.1
MASKED = -1e30

RING = 4
ID_BITS = 4


def block_causal_attention_and_moe(
    nc: bass.Bass, x, Wq, Wk, Wv, centroids, gate_bias, wg_s, wu_s, wd_s, wg, wu, wd, out
):
    B, S, D = x.shape
    E, _, I = wg.shape
    TILES = B * S // P
    BT = S // P
    KC = D // P
    HALVES = wg_s.shape[1] // I
    assert D == 256 and I == P and BT == 4 and E == 16 and HALVES == 2
    SCALE = float(D) ** -0.5
    SHARED_STEPS = TILES * HALVES
    EXPERT_TILES = 2 * TILES + E
    GROUPS = EXPERT_TILES // RING
    SLOTS = EXPERT_TILES * P
    ROW = D + 2
    WE = KC * 2 * I + D
    RESULTS = 2 * TILES * P

    expert_rows = nc.dram_tensor("expert_rows", (SLOTS, ROW), F32, kind="Internal").ap()
    expert_out = nc.dram_tensor("expert_out", (RESULTS, D), F32, kind="Internal").ap()

    ctx = ExitStack()
    with ctx:
        def sb(name, shape, dt=F32):
            return ctx.enter_context(nc.sbuf_tensor(name, shape, dt))

        def sem(name):
            return ctx.enter_context(nc.semaphore(name))

        res = sb("res", [P, TILES, D])
        rows2 = sb("rows2", [P, TILES, ROW])
        w_hi = sb("w_hi", [P, E + HALVES, WE], F32R)
        w_lo = sb("w_lo", [P, E + HALVES, WE], F32R)
        w_raw = sb("w_raw", [P, 2, WE])
        ident = sb("ident", [P, P])
        ident_b = sb("ident_b", [P, P], BF16)
        mask_b = sb("mask_b", [P, P], BF16)
        before_b = sb("before_b", [P, P], BF16)
        ones_b = sb("ones_b", [P, P], BF16)
        template = sb("template", [P, ROW])
        a_hi = sb("a_hi", [P, KC, D], F32R)
        a_lo = sb("a_lo", [P, KC, D], F32R)
        wv_raw = sb("wv_raw", [P, KC, D])
        wv_hi = sb("wv_hi", [P, KC, D], F32R)
        wv_lo = sb("wv_lo", [P, KC, D], F32R)
        cen_raw = sb("cen_raw", [E, D])
        cen_hi = sb("cen_hi", [P, KC, E], F32R)
        cen_lo = sb("cen_lo", [P, KC, E], F32R)
        stats = sb("stats", [P, 2, BT, 6])
        mv = sb("mv", [P, 2, BT, 2])
        veps = sb("veps", [P, 2, BT])
        rstd = sb("rstd", [P, 2, BT])
        minus_half = sb("minus_half", [P, BT])
        smax = sb("smax", [P, BT])
        nbias = sb("nbias", [P, BT])
        rsum = sb("rsum", [P, BT])
        rinv = sb("rinv", [P, BT])
        en = sb("en", [P, TILES, E])
        logit = sb("logit", [P, BT, E])
        bias_all = sb("bias_all", [P, E])
        iota_u = sb("iota_u", [P, EXPERT_TILES], I32)
        ones_e = sb("ones_e", [P, E])
        weight = sb("weight", [P, 2, TILES])

        with ExitStack() as attention:
            def asb(name, shape, dt=F32):
                return attention.enter_context(nc.sbuf_tensor(name, shape, dt))

            xn = asb("xn", [P, BT, D])
            x2 = asb("x2", [P, BT, D])
            probs = asb("probs", [P, 2, S])
            wqkT = x2[:].rearrange("p (w c) n -> p w c n", w=2)
            wqk_raw = probs[:].rearrange("p w (c n) -> p w c n", c=KC)
            xT_hi = asb("xT_hi", [P, KC, S], F32R)
            xT_lo = asb("xT_lo", [P, KC, S], F32R)
            qT_hi = asb("qT_hi", [P, KC, S], F32R)
            qT_lo = asb("qT_lo", [P, KC, S], F32R)
            v_hi = asb("v_hi", [P, BT, D], F32R)
            v_lo = asb("v_lo", [P, BT, D], F32R)
            pT_hi = asb("pT_hi", [P, 2, S], F32R)
            pT_lo = asb("pT_lo", [P, 2, S], F32R)
            x2T_hi, x2T_lo = pT_hi, pT_lo

        aff = sb("aff", [P, TILES, E])
        biased = sb("biased", [P, TILES, E])
        top8 = sb("top8", [P, TILES, 8])
        top8_at = sb("top8_at", [P, TILES, 8], U32)
        top_at = sb("top_at", [P, TILES, 2])
        iota_f = sb("iota_f", [P, EXPERT_TILES])
        hot = sb("hot", [P, 2, TILES, E])
        picked = sb("picked", [P, TILES, E])
        hot_b = sb("hot_b", [P, TILES + 1, E], BF16)
        taff = sb("taff", [P, 2, TILES])
        tsum = sb("tsum", [P, TILES])
        pos = sb("pos", [P, TILES, E])
        slot_f = sb("slot_f", [P, 2, TILES])
        slot_u = sb("slot_u", [P, 2, TILES], U32)
        cnt = sb("cnt", [P, E])
        cnt_i = sb("cnt_i", [P, E], I32)
        tiles_f = sb("tiles_f", [P, E])
        ends = sb("ends", [P, E])
        base = sb("base", [P, E])
        past = sb("past", [1, EXPERT_TILES, E])
        tile_expert = sb("tile_expert", [1, EXPERT_TILES])
        digit = sb("digit", [1, RING])
        shifted = sb("shifted", [1, GROUPS, RING])
        word_f = sb("word_f", [1, GROUPS])
        word = sb("word", [1, GROUPS], U32)
        ring = sb("ring", [P, RING, ROW])
        dest = sb("dest", [P, RING], U32)
        gT_hi = sb("gT_hi", [P, 2, D], F32R)
        gT_lo = sb("gT_lo", [P, 2, D], F32R)
        sg = sb("sg", [P, 2, I])
        h = sb("h", [P, 2, I])
        hT_hi = sb("hT_hi", [P, 2, P], F32R)
        hT_lo = sb("hT_lo", [P, 2, P], F32R)
        y_sb = sb("y_sb", [P, RING, D])
        both = sb("both", [P, 2, 2, D])
        fin = sb("fin", [P, 2, D])

        bank = ctx.enter_context(nc.psum_tensor("bank", [P, 8, 512], F32))

        ld_wqk = sem("ld_wqk"); ld_wv = sem("ld_wv"); ld_cen = sem("ld_cen"); ld_bias = sem("ld_bias")
        ld_x = [sem(f"ld_x{b}") for b in range(B)]
        ld_w = [sem(f"ld_w{k}") for k in range(2)]
        filled = sem("filled")
        c_step = sem("c_step")
        consts = sem("consts")
        const_b = sem("const_b")
        w_split = sem("w_split")
        wT_done = sem("wT_done"); wT_copied = sem("wT_copied"); a_done = sem("a_done")
        a_hi_done = sem("a_hi_done"); a_lo_done = sem("a_lo_done"); wv_done = sem("wv_done")
        cenT = sem("cenT"); cen_hi_done = sem("cen_hi_done"); cen_done = sem("cen_done")
        ln1_stats = sem("ln1_stats"); ln1_mv = sem("ln1_mv"); ln1_ve = sem("ln1_ve"); ln1_rstd = sem("ln1_rstd")
        ln1_done = sem("ln1_done")
        ln2_stats = sem("ln2_stats"); ln2_mv = sem("ln2_mv"); ln2_ve = sem("ln2_ve"); ln2_rstd = sem("ln2_rstd")
        ln2_done = sem("ln2_done"); rows_done = sem("rows_done")
        pe_xT = sem("pe_xT"); a_xT = sem("a_xT"); d_xT = sem("d_xT")
        pe_qT = sem("pe_qT"); a_qT = sem("a_qT"); d_qT = sem("d_qT")
        pe_v = sem("pe_v"); a_v = sem("a_v"); d_v = sem("d_v")
        pe_s = sem("pe_s"); d_max = sem("d_max"); d_nbias = sem("d_nbias"); a_exp = sem("a_exp")
        pe_pT = sem("pe_pT"); a_pT = sem("a_pT"); d_pT = sem("d_pT")
        pe_o = sem("pe_o"); d_rinv = sem("d_rinv"); d_o = sem("d_o")
        pe_x2T = sem("pe_x2T"); a_x2T = sem("a_x2T"); d_x2T = sem("d_x2T")
        pe_logit = sem("pe_logit"); d_logit = sem("d_logit"); a_en = sem("a_en")
        apart = sem("apart")
        r_step = sem("r_step")
        hot_done = sem("hot_done"); ranks = sem("ranks"); slots_done = sem("slots_done"); words_done = sem("words_done")
        ids0 = sem("ids0"); ids1 = sem("ids1"); sent = [sem("sent0"), sem("sent1")]
        ld_t = [sem(f"ld_t{k}") for k in range(RING)]
        pe_t = sem("pe_t"); a_t = sem("a_t"); d_t = sem("d_t"); d_dest = sem("d_dest")
        pe_gu = sem("pe_gu"); a_silu = sem("a_silu"); d_h = sem("d_h")
        pe_hT = sem("pe_hT"); a_hT = sem("a_hT"); d_hT = sem("d_hT")
        pe_y = sem("pe_y"); d_y = sem("d_y")
        sc_y = [sem(f"sc_y{k}") for k in range(RING)]
        ld_both = [sem(f"ld_both{k}") for k in range(2)]
        f_part = sem("f_part"); f_done = sem("f_done")
        stored = [sem(f"stored{k}") for k in range(2)]

        x_v = x.rearrange("b (t p) d -> b p t d", p=P)
        out_v = out.rearrange("b (t p) d -> (b t) p d", p=P)
        both_v = expert_out.rearrange("(t p c) d -> t p c d", p=P, c=2)

        def need(eng, s, v):
            if not isinstance(v, int) or v > 0:
                eng.wait_ge(s, v)

        def wait_apart(eng, s, v):
            eng.wait_ge(s, v)
            if not isinstance(v, int):
                eng.sem_inc(apart, 1)

        def over_batches(eng, body, after=None):
            body(0, first=True, last=False)
            with eng.Fori(1, B - 1) as b:
                body(b, first=False, last=False)
            body(B - 1, first=False, last=True)

        def pipelined(eng, q0, groups, stages):
            n = RING * groups

            def group(q, first, last, extra=0):
                for k in range(RING + extra):
                    for lag, f in stages:
                        kk = k + lag
                        if first and kk < 0:
                            continue
                        if last and kk >= RING:
                            continue
                        if last and k >= RING and kk < 0:
                            continue
                        f(q + kk // RING, kk % RING)

            for lag, f in stages:
                for k in range(max(lag, 0)):
                    f(q0 + k // RING, k % RING)
            group(q0, True, False)
            with eng.Fori(q0 + 1, q0 + groups - 1) as q:
                group(q, False, False)
            group(q0 + groups - 1, False, True, extra=2)

        q_shared, q_routed = 0, SHARED_STEPS // RING

        def split3(pe, acc, hi, lo, rhi, rlo, first, last):
            pe.matmul(acc, lo, rhi, start=first, stop=False)
            pe.matmul(acc, hi, rlo, start=False, stop=False)
            return pe.matmul(acc, hi, rhi, start=False, stop=last)

        block = ctx.enter_context(nc.Block())

        @block.sync
        def _(sp):
            sp.dma_start(res[:, 0:BT, :], x_v[0]).then_inc(ld_x[0], 16)
            for n, w in enumerate((Wq, Wk)):
                sp.dma_start(wqk_raw[:, n], w.rearrange("(c p) n -> p c n", p=P)).then_inc(ld_wqk, 16)
            sp.dma_start(wv_raw[:], Wv.rearrange("(c p) n -> p c n", p=P)).then_inc(ld_wv, 16)
            sp.dma_start(cen_raw[:], centroids).then_inc(ld_cen, 16)
            for b in range(1, B):
                sp.dma_start(res[:, b * BT:(b + 1) * BT, :], x_v[b]).then_inc(ld_x[b], 16)
            sp.dma_start(bias_all[:], gate_bias.rearrange("(a e) -> a e", a=1).broadcast_to([P, E])).then_inc(ld_bias, 16)

            def gate_up(k, half):
                return w_raw[:, k, 0:KC * 2 * I].rearrange("p (c n) -> p c n", c=KC)[:, :, half * I:(half + 1) * I]

            def load_experts(m):
                for k in range(2):
                    e = 2 * m + k
                    need(sp, w_split, 4 * m)
                    for half, w in enumerate((wg, wu)):
                        sp.dma_start(gate_up(k, half), w[bass.ds(e, 1)].rearrange("a (c p) i -> p (a c) i", p=P)).then_inc(ld_w[k], 16)
                    sp.dma_start(w_raw[:, k, KC * 2 * I:WE], wd[bass.ds(e, 1)].rearrange("a p d -> p (a d)")).then_inc(ld_w[k], 16)

            load_experts(0)
            with sp.Fori(1, E // 2) as m:
                load_experts(m)
            for k in range(HALVES):
                sp.wait_ge(w_split, 2 * E)
                for half, w in enumerate((wg_s, wu_s)):
                    sp.dma_start(gate_up(k, half), w[:, k * I:(k + 1) * I].rearrange("(c p) i -> p c i", p=P)).then_inc(ld_w[k], 16)
                sp.dma_start(w_raw[:, k, KC * 2 * I:WE], wd_s[k * I:(k + 1) * I, :]).then_inc(ld_w[k], 16)

            sp.wait_ge(consts, 1)
            for j in range(EXPERT_TILES):
                sp.dma_start(expert_rows[j * P:(j + 1) * P, :], template[:]).then_inc(filled, 16)

            def load_shared(q, k):
                need(sp, pe_t, RING * (q - 1) + k + 1)
                sp.dma_start(ring[:, k, 0:D], rows2[:, bass.ds(2 * q + k // 2, 1), 0:D]).then_inc(ld_t[k], 16)

            sp.wait_ge(rows_done, B)
            for k in range(RING):
                load_shared(0, k)
            with sp.Fori(1, q_routed) as q:
                for k in range(RING):
                    load_shared(q, k)

            def load_routed(q, k):
                if not isinstance(q, int):
                    wait_apart(sp, d_dest, RING * (q - 1 - q_routed) + k + 1)
                wait_apart(sp, pe_t, RING * (q - 1) + k + 1)
                sp.dma_start(ring[:, k, :], expert_rows[bass.ds((RING * (q - q_routed) + k) * P, P), :]).then_inc(ld_t[k], 16)

            for s in sent:
                sp.wait_ge(s, 16 * TILES)
            for k in range(RING):
                load_routed(q_routed, k)
            with sp.Fori(q_routed + 1, q_routed + GROUPS) as q:
                for k in range(RING):
                    load_routed(q, k)

            for k in range(RING):
                sp.wait_ge(sc_y[k], 16 * GROUPS)

            def load_both(m, k, first):
                t = 2 * m + k
                if not first:
                    sp.wait_ge(f_done, t - 1)
                sp.dma_start(both[:, k], both_v[bass.ds(t, 1)].rearrange("t p c d -> p (t c) d")).then_inc(ld_both[k], 16)

            def store(m, k):
                t = 2 * m + k
                sp.wait_ge(f_done, t + 1)
                sp.dma_start(out_v[bass.ds(t, 1)].rearrange("t p d -> p (t d)"), fin[:, k, :]).then_inc(stored[k], 16)

            for k in range(2):
                load_both(0, k, True)
            with sp.Fori(1, TILES // 2) as m:
                for k in range(2):
                    store(m - 1, k)
                    load_both(m, k, False)
            for k in range(2):
                store(TILES // 2 - 1, k)
            for k in range(2):
                sp.wait_ge(stored[k], 16 * TILES // 2)

        @block.gpsimd
        def _(pool):
            g = nc.gpsimd
            done = [0]

            def step(ins):
                done[0] += 1
                ins.then_inc(c_step, 1)
                pool.wait_ge(c_step, done[0])

            step(g.memset(ident[:], 0.0))
            step(g.affine_select(out=ident[:], in_=ident[:], compare_op=ALU.not_equal, fill=1.0, base=0,
                                 pattern=[[-1, P]], channel_multiplier=1))
            step(g.memset(minus_half[:], -0.5))
            step(g.memset(mask_b[:], 0.0))
            step(g.affine_select(out=mask_b[:], in_=mask_b[:], compare_op=ALU.is_ge, fill=MASKED, base=0,
                                 pattern=[[-1, P]], channel_multiplier=1))
            step(g.memset(before_b[:], 1.0))
            step(g.affine_select(out=before_b[:], in_=before_b[:], compare_op=ALU.is_gt, fill=0.0, base=0,
                                 pattern=[[1, P]], channel_multiplier=-1))
            step(g.memset(ones_b[:], 1.0))
            step(g.memset(template[:], 0.0))
            step(g.iota(template[:, D:D + 1].bitcast(U32), pattern=[[0, 1]], base=RESULTS, channel_multiplier=1))
            step(g.memset(rows2[:, :, D + 1:ROW], 0.0))
            step(g.iota(rows2[:, :, D:D + 1].bitcast(U32), pattern=[[2 * P, TILES], [0, 1]], base=0, channel_multiplier=2))
            step(g.iota(iota_u[:], pattern=[[1, EXPERT_TILES]], base=0, channel_multiplier=0))
            step(g.tensor_copy(ident_b[:], ident[:]))
            g.memset(ones_e[:], 1.0).then_inc(consts, 1)

            def rsqrt(n, b, mv_ready, added, ready):
                wait_apart(pool, mv_ready, b + 1)
                g.tensor_scalar(veps[:, n, :], mv[:, n, :, 1], LN_EPS, None, ALU.add).then_inc(added, 1)
                pool.wait_ge(added, b + 1)
                g.tensor_tensor(rstd[:, n, :], veps[:, n, :], minus_half[:], ALU.pow).then_inc(ready, 1)

            def split_weights(e, k, nth):
                wait_apart(pool, ld_w[k], 48 * (nth + 1))
                g.tensor_copy(w_hi[:, bass.ds(e, 1), :], w_raw[:, k:k + 1, :]).then_inc(w_split, 1)
                wait_apart(pool, w_split, 2 * e + 1)
                g.tensor_tensor(w_lo[:, bass.ds(e, 1), :], w_raw[:, k:k + 1, :],
                                w_hi[:, bass.ds(e, 1), :].bitcast(F32), ALU.subtract).then_inc(w_split, 1)

            rsqrt(0, 0, ln1_mv, ln1_ve, ln1_rstd)

            def batch(b, first, last):
                for n in range(2):
                    split_weights(4 * b + n, n, 2 * b)
                if not last:
                    rsqrt(0, b + 1, ln1_mv, ln1_ve, ln1_rstd)
                for n in range(2):
                    split_weights(4 * b + 2 + n, n, 2 * b + 1)
                rsqrt(1, b, ln2_mv, ln2_ve, ln2_rstd)

            over_batches(pool, batch)
            for n in range(HALVES):
                split_weights(E + n, n, E // 2)

            pool.wait_ge(slots_done, 1)
            pool.wait_ge(rows_done, B)
            pool.wait_ge(filled, 16 * EXPERT_TILES)
            for c in range(2):
                if c:
                    pool.wait_ge(ids1, 1)
                for t in range(TILES):
                    g.indirect_dma_start(expert_rows, bass.IndirectOffsetOnAxis(slot_u[:, c, t:t + 1], 0),
                                         rows2[:, t, :], None).then_inc(sent[c], 16)

            def scatter_results(q, k):
                wait_apart(pool, d_y, RING * q + k + 1)
                g.indirect_dma_start(expert_out, bass.IndirectOffsetOnAxis(dest[:, k:k + 1], 0),
                                     y_sb[:, k, :], None, bounds_check=RESULTS - 1, oob_is_err=False).then_inc(sc_y[k], 16)

            with pool.Fori(q_routed, q_routed + GROUPS) as q:
                for k in range(RING):
                    scatter_results(q, k)

        @block.scalar
        def _(act):
            a = nc.scalar
            act.wait_ge(ld_wv, 16)
            a.activation(wv_hi[:], wv_raw[:], ACT.Copy).then_inc(wv_done, 1)
            for n in range(2):
                act.wait_ge(wT_done, n + 1)
                a.activation(wqkT[:, n].rearrange("p c n -> p (c n)"), bank[:, n, :], ACT.Copy).then_inc(wT_copied, 1)
            act.wait_ge(a_done, 1)
            a.activation(a_hi[:].rearrange("p c n -> p (c n)"), bank[:, 2, :], ACT.Copy).then_inc(a_hi_done, 1)
            act.wait_ge(cenT, 1)
            a.activation(cen_hi[:], bank[:, 3, 0:KC * E].rearrange("p (c e) -> p c e", c=KC),
                         ACT.Copy).then_inc(cen_hi_done, 1)

            def transposed(b, made, mine, hi, freed, freed_at):
                need(act, freed, freed_at)
                for c in range(KC):
                    act.wait_ge(made, KC * b + c + 1)
                    a.activation(hi[:, c, :], bank[:, c, :], ACT.Copy).then_inc(mine, 1)

            def gates(b):
                act.wait_ge(d_logit, 2 * (b + 1))
                a.activation(en[:, bass.ds(BT * b, BT), :], logit[:],
                             ACT.Exp, scale=-1.0).then_inc(a_en, 1)

            def batch(b, first, last):
                transposed(b, pe_xT, a_xT, xT_hi, pe_s, BT * b)
                for m in range(KC):
                    act.wait_ge(pe_qT, KC * b + m + 1)
                    a.activation(qT_hi[:, m, :], bank[:, 2 + m, :], ACT.Copy).then_inc(a_qT, 1)
                need(act, pe_o, BT * b)
                for n in range(2):
                    act.wait_ge(pe_v, 2 * b + n + 1)
                    a.activation(v_hi[:, 2 * n:2 * n + 2, :].rearrange("p t d -> p (t d)"), bank[:, 4 + n, :],
                                 ACT.Copy).then_inc(a_v, 1)
                if not first:
                    transposed(b - 1, pe_x2T, a_x2T, x2T_hi, pe_o, BT * b)

                def exps(i):
                    act.wait_ge(d_nbias, BT * b + i + 1)
                    need(act, pe_pT, BT * b + max(i - 1, 0))
                    n = (i + 1) * P
                    a.activation(probs[:, i % 2, 0:n], bank[:, 6 + i % 2, 0:n], ACT.Exp, bias=nbias[:, i:i + 1],
                                 scale=SCALE, accum_out=rsum[:, i:i + 1]).then_inc(a_exp, 1)

                def probsT(i):
                    act.wait_ge(pe_pT, BT * b + i + 1)
                    need(act, pe_o, BT * b + max(i - 1, 0))
                    n = (i + 1) * P
                    a.activation(pT_hi[:, i % 2, 0:n], bank[:, i % 2, 0:n], ACT.Copy).then_inc(a_pT, 1)

                exps(0)
                exps(1)
                if not first:
                    gates(b - 1)
                probsT(0)
                exps(2)
                probsT(1)
                exps(3)
                probsT(2)
                probsT(3)

            over_batches(act, batch)
            transposed(B - 1, pe_x2T, a_x2T, x2T_hi, pe_o, BT * B)
            gates(B - 1)

            def tile_hi(q, k):
                J = RING * q + k
                act.wait_ge(pe_t, J + 1)
                need(act, pe_gu, J - 1)
                a.activation(gT_hi[:, k % 2, :], bank[:, k % 2, 0:D], ACT.Copy).then_inc(a_t, 1)

            def silu(q, k):
                J = RING * q + k
                act.wait_ge(pe_gu, J + 1)
                need(act, d_h, J - 1)
                a.activation(sg[:, k % 2, :], bank[:, 2 + k % 2, 0:I], ACT.Silu).then_inc(a_silu, 1)

            def hidden_hi(q, k):
                J = RING * q + k
                act.wait_ge(pe_hT, J + 1)
                need(act, pe_y, J - 1)
                a.activation(hT_hi[:, k % 2, :], bank[:, 4 + k % 2, 0:P], ACT.Copy).then_inc(a_hT, 1)

            stages = [(1, tile_hi), (0, silu), (-1, hidden_hi)]
            pipelined(act, q_shared, SHARED_STEPS // RING, stages)
            pipelined(act, q_routed, GROUPS, stages)

        @block.vector
        def _(dve):
            v = nc.vector

            def layernorm(n, b, src, dst, stat, mvs, ready, done, dst_free, free_at):
                for t in range(BT):
                    ins = v.bn_stats(stats[:, n, t, :], src(t))
                ins.then_inc(stat, 1)
                wait_apart(dve, stat, b + 1)
                for t in range(BT):
                    ins = v.bn_aggr(mv[:, n, t, :], stats[:, n, t, :])
                ins.then_inc(mvs, 1)
                dve.wait_ge(ready, b + 1)
                need(dve, dst_free, free_at)
                for t in range(BT):
                    v.tensor_scalar(dst[:, t, :], src(t), mv[:, n, t, 0:1], rstd[:, n, t:t + 1],
                                    ALU.subtract, ALU.mult).then_inc(done, 1)

            def res_tile(b, t):
                return res[:, bass.ds(BT * b + t, 1), :].rearrange("p a d -> p (a d)") if not isinstance(b, int) \
                    else res[:, BT * b + t, :]

            def ln1(b):
                layernorm(0, b, lambda t: res_tile(b, t), xn, ln1_stats, ln1_mv, ln1_rstd, ln1_done, pe_xT, KC * b)

            def sub(dst, src, hi):
                return v.tensor_tensor(dst, src, hi.bitcast(F32), ALU.subtract)

            dve.wait_ge(ld_x[0], 16)
            ln1(0)
            dve.wait_ge(wv_done, 1)
            sub(wv_lo[:], wv_raw[:], wv_hi[:]).then_inc(wv_done, 1)
            dve.wait_ge(a_hi_done, 1)
            sub(a_lo[:].rearrange("p c n -> p (c n)"), bank[:, 2, :], a_hi[:].rearrange("p c n -> p (c n)")).then_inc(a_lo_done, 1)
            dve.wait_ge(cen_hi_done, 1)
            sub(cen_lo[:], bank[:, 3, 0:KC * E].rearrange("p (c e) -> p c e", c=KC),
                cen_hi[:]).then_inc(cen_done, 1)

            def transposed(b, his, mine, lo, hi, freed, freed_at):
                need(dve, freed, freed_at)
                for c in range(KC):
                    dve.wait_ge(his, KC * b + c + 1)
                    sub(lo[:, c, :], bank[:, c, :], hi[:, c, :]).then_inc(mine, 1)

            def clamped(b):
                need(dve, a_en, b)
                for n in range(2):
                    dve.wait_ge(pe_logit, 2 * b + n + 1)
                    v.tensor_scalar(logit[:, 2 * n:2 * n + 2, :],
                                    bank[:, 4 + n, :].rearrange("p (t n) -> p t n", t=2)[:, :, 0:E],
                                    LEAST_LOGIT, None, ALU.max).then_inc(d_logit, 1)

            def batch(b, first, last):
                transposed(b, a_xT, d_xT, xT_lo, xT_hi, pe_s, BT * b)
                for m in range(KC):
                    dve.wait_ge(a_qT, KC * b + m + 1)
                    sub(qT_lo[:, m, :], bank[:, 2 + m, :], qT_hi[:, m, :]).then_inc(d_qT, 1)
                need(dve, pe_o, BT * b)
                for n in range(2):
                    dve.wait_ge(a_v, 2 * b + n + 1)
                    sub(v_lo[:, 2 * n:2 * n + 2, :].rearrange("p t d -> p (t d)"), bank[:, 4 + n, :],
                        v_hi[:, 2 * n:2 * n + 2, :].rearrange("p t d -> p (t d)")).then_inc(d_v, 1)
                if not first:
                    transposed(b - 1, a_x2T, d_x2T, x2T_lo, x2T_hi, pe_o, BT * b)

                def row_max(i):
                    dve.wait_ge(pe_s, BT * b + i + 1)
                    v.reduce_max(smax[:, i:i + 1], bank[:, 6 + i % 2, 0:(i + 1) * P], AX).then_inc(d_max, 1)
                    dve.wait_ge(d_max, BT * b + i + 1)
                    v.tensor_scalar(nbias[:, i:i + 1], smax[:, i:i + 1], -SCALE, None, ALU.mult).then_inc(d_nbias, 1)

                def probsT(i):
                    dve.wait_ge(a_pT, BT * b + i + 1)
                    need(dve, pe_o, BT * b + max(i - 1, 0))
                    n = (i + 1) * P
                    sub(pT_lo[:, i % 2, 0:n], bank[:, i % 2, 0:n], pT_hi[:, i % 2, 0:n]).then_inc(d_pT, 1)

                def attended(i):
                    dve.wait_ge(a_exp, BT * b + i + 1)
                    v.reciprocal(rinv[:, i:i + 1], rsum[:, i:i + 1]).then_inc(d_rinv, 1)
                    dve.wait_ge(d_rinv, BT * b + i + 1)
                    dve.wait_ge(pe_o, BT * b + i + 1)
                    r = res_tile(b, i)
                    v.scalar_tensor_tensor(out=r, in0=bank[:, 2 + i % 2, 0:D], scalar=rinv[:, i:i + 1], in1=r,
                                           op0=ALU.mult, op1=ALU.add).then_inc(d_o, 1)

                row_max(0)
                row_max(1)
                if not first:
                    clamped(b - 1)
                probsT(0)
                row_max(2)
                probsT(1)
                attended(0)
                row_max(3)
                probsT(2)
                attended(1)
                probsT(3)
                if not last:
                    if first:
                        dve.wait_ge(ld_x[1], 16)
                    else:
                        for n in range(2, B):
                            dve.wait_ge(ld_x[n], 16)
                    ln1(b + 1)
                attended(2)
                attended(3)
                wait_apart(dve, d_o, BT * (b + 1))
                layernorm(1, b, lambda t: res_tile(b, t), x2, ln2_stats, ln2_mv, ln2_rstd, ln2_done, pe_x2T, KC * b)
                dve.wait_ge(ln2_done, BT * (b + 1))
                dve.wait_ge(consts, 1)
                v.tensor_copy(rows2[:, bass.ds(BT * b, BT), 0:D] if not isinstance(b, int)
                              else rows2[:, BT * b:BT * (b + 1), 0:D], x2[:]).then_inc(rows_done, 1)

            over_batches(dve, batch)
            transposed(B - 1, a_x2T, d_x2T, x2T_lo, x2T_hi, pe_o, BT * B)
            clamped(B - 1)

            n_step = [0]

            def step(ins):
                n_step[0] += 1
                ins.then_inc(r_step, 1)
                dve.wait_ge(r_step, n_step[0])

            def over_e(ap):
                return ap.unsqueeze(2).broadcast_to([P, TILES, E])

            def over_t(ap):
                return ap.unsqueeze(1).broadcast_to([P, TILES, E])

            dve.wait_ge(a_en, B)
            dve.wait_ge(ld_bias, 16)
            step(v.tensor_scalar(en[:], en[:], 1.0, None, ALU.add))
            step(v.reciprocal(aff[:], en[:]))
            step(v.tensor_tensor(biased[:], aff[:], over_t(bias_all[:]), ALU.add))
            for t in range(TILES):
                ins = v.max(top8[:, t, :], biased[:, t, :])
            step(ins)
            for t in range(TILES):
                ins = v.max_index(top8_at[:, t, :], top8[:, t, :], biased[:, t, :])
            step(ins)
            v.tensor_copy(iota_f[:], iota_u[:])
            step(v.tensor_copy(top_at[:], top8_at[:, :, 0:2]))
            for c in range(2):
                ins = v.tensor_tensor(hot[:, c], over_t(iota_f[:, 0:E]), over_e(top_at[:, :, c]), ALU.is_equal)
            step(ins)
            v.memset(hot_b[:, TILES, :], 0.0).then_inc(hot_done, 1)
            v.tensor_tensor(hot_b[:, 0:TILES, :], hot[:, 0], hot[:, 1], ALU.add).then_inc(hot_done, 1)
            for c in range(2):
                step(v.tensor_tensor(picked[:], hot[:, c], aff[:], ALU.mult))
                step(v.tensor_reduce(taff[:, c], picked[:], AX, ALU.add))
            dve.wait_ge(ranks, 1)
            step(v.tensor_scalar(cnt[:], bank[:, 0, TILES * E:(TILES + 1) * E], float(P - 1), None, ALU.add))
            step(v.tensor_copy(cnt_i[:], cnt[:]))
            step(v.tensor_scalar(cnt_i[:], cnt_i[:], P.bit_length() - 1, None, ALU.arith_shift_right))
            step(v.tensor_copy(tiles_f[:], cnt_i[:]))
            step(v.tensor_tensor_scan(ends[:], ones_e[:], tiles_f[:], 0.0, ALU.mult, ALU.add))
            step(v.tensor_tensor(base[:], ends[:], tiles_f[:], ALU.subtract))
            step(v.tensor_scalar(base[:], base[:], float(P), None, ALU.mult))
            step(v.tensor_tensor(pos[:], bank[:, 0, 0:TILES * E].rearrange("p (t e) -> p t e", t=TILES),
                                 over_t(base[:]), ALU.add))
            for c in range(2):
                step(v.tensor_tensor(picked[:], hot[:, c], pos[:], ALU.mult))
                step(v.tensor_reduce(slot_f[:, c], picked[:], AX, ALU.add))
            v.tensor_copy(slot_u[:], slot_f[:]).then_inc(slots_done, 1)
            step(v.tensor_tensor(past[:], ends[0:1, :].unsqueeze(1).broadcast_to([1, EXPERT_TILES, E]),
                                 iota_f[0:1, :].unsqueeze(2).broadcast_to([1, EXPERT_TILES, E]), ALU.is_le))
            step(v.tensor_reduce(tile_expert[:], past[:], AX, ALU.add))
            step(v.tensor_scalar(tile_expert[:], tile_expert[:], float(E - 1), None, ALU.min))
            for k in range(RING):
                ins = v.memset(digit[:, k:k + 1], float(1 << (ID_BITS * k)))
            step(ins)
            step(v.tensor_tensor(shifted[:], tile_expert[:].rearrange("a (g k) -> a g k", k=RING),
                                 digit[:].unsqueeze(1).broadcast_to([1, GROUPS, RING]), ALU.mult))
            step(v.tensor_reduce(word_f[:], shifted[:], AX, ALU.add))
            v.tensor_copy(word[:], word_f[:]).then_inc(words_done, 1)
            step(v.tensor_tensor(tsum[:], taff[:, 0], taff[:, 1], ALU.add))
            step(v.tensor_scalar(tsum[:], tsum[:], GATE_EPS, None, ALU.add))
            step(v.reciprocal(tsum[:], tsum[:]))
            for c in range(2):
                ins = v.tensor_tensor(weight[:, c], taff[:, c], tsum[:], ALU.mult)
            step(ins)
            dve.wait_ge(sent[0], 16 * TILES)
            ids = rows2[:, :, D:D + 1].bitcast(U32)
            v.tensor_scalar(ids, ids, 1.0, None, ALU.add).then_inc(ids1, 1)

            def tile_lo(q, k):
                J = RING * q + k
                dve.wait_ge(a_t, J + 1)
                need(dve, pe_gu, J - 1)
                sub(gT_lo[:, k % 2, :], bank[:, k % 2, 0:D], gT_hi[:, k % 2, :]).then_inc(d_t, 1)

            def tile_lo_routed(q, k):
                tile_lo(q, k)
                need(dve, sc_y[k], 16 * (q - q_routed))
                v.tensor_copy(dest[:, k:k + 1], ring[:, k, D:D + 1].bitcast(U32)).then_inc(d_dest, 1)

            def hidden(q, k):
                J = RING * q + k
                dve.wait_ge(a_silu, J + 1)
                need(dve, pe_hT, J - 1)
                v.tensor_tensor(h[:, k % 2, :], sg[:, k % 2, :], bank[:, 2 + k % 2, I:2 * I], ALU.mult).then_inc(d_h, 1)

            def hidden_lo(q, k):
                J = RING * q + k
                dve.wait_ge(a_hT, J + 1)
                need(dve, pe_y, J - 1)
                sub(hT_lo[:, k % 2, :], bank[:, 4 + k % 2, 0:P], hT_hi[:, k % 2, :]).then_inc(d_hT, 1)

            def add_shared(q, k):
                J = RING * q + k
                dve.wait_ge(pe_y, J + 1)
                need(dve, d_y, J)
                r = res[:, bass.ds(2 * q + k // 2, 1), :].rearrange("p a d -> p (a d)")
                v.scalar_tensor_tensor(out=r, in0=bank[:, 6 + k % 2, 0:D], scalar=SHARED_RATIO, in1=r,
                                       op0=ALU.mult, op1=ALU.add).then_inc(d_y, 1)

            def keep_results(q, k):
                J = RING * q + k
                dve.wait_ge(pe_y, J + 1)
                v.tensor_copy(y_sb[:, k, :], bank[:, 6 + k % 2, 0:D]).then_inc(d_y, 1)

            pipelined(dve, q_shared, SHARED_STEPS // RING, [(1, tile_lo), (0, hidden), (-1, hidden_lo), (-2, add_shared)])
            pipelined(dve, q_routed, GROUPS, [(1, tile_lo_routed), (0, hidden), (-1, hidden_lo), (-2, keep_results)])

            def combine(m, k):
                t = 2 * m + k
                dve.wait_ge(ld_both[k], 16 * (m + 1))
                need(dve, stored[k], 16 * m)
                w = [weight[:, c, bass.ds(t, 1)] for c in range(2)]
                v.scalar_tensor_tensor(out=fin[:, k, :], in0=both[:, k, 0, :], scalar=w[0],
                                       in1=res[:, bass.ds(t, 1), :].rearrange("p a d -> p (a d)"),
                                       op0=ALU.mult, op1=ALU.add).then_inc(f_part, 1)
                dve.wait_ge(f_part, t + 1)
                v.scalar_tensor_tensor(out=fin[:, k, :], in0=both[:, k, 1, :], scalar=w[1], in1=fin[:, k, :],
                                       op0=ALU.mult, op1=ALU.add).then_inc(f_done, 1)

            for k in range(2):
                combine(0, k)
            with dve.Fori(1, TILES // 2) as m:
                for k in range(2):
                    combine(m, k)

        @block.tensor
        def _(pe):
            pe.wait_ge(ld_wqk, 32)
            pe.wait_ge(consts, 1)
            for n in range(2):
                for c in range(KC):
                    for r in range(KC):
                        ins = pe.transpose(bank[:, n, c * D + r * P:c * D + (r + 1) * P],
                                           wqk_raw[:, n, r, c * P:(c + 1) * P], ident[:])
                ins.then_inc(wT_done, 1)
            pe.wait_ge(ld_cen, 16)
            for c in range(KC):
                ins = pe.transpose(bank[:, 3, c * E:(c + 1) * E], cen_raw[:, c * P:(c + 1) * P], ident[0:E, 0:E])
            ins.then_inc(cenT, 1)
            pe.wait_ge(wT_copied, 2)
            for r in range(KC):
                for c in range(KC):
                    ins = pe.matmul(bank[:, 2, r * D:(r + 1) * D], wqkT[:, 0, c, r * P:(r + 1) * P], wqkT[:, 1, c, :],
                                    start=(c == 0), stop=(c == KC - 1))
            ins.then_inc(a_done, 1)
            pe.wait_ge(a_lo_done, 1)
            pe.wait_ge(wv_done, 2)
            pe.wait_ge(cen_done, 1)

            def transpose_rows(src, made):
                for c in range(KC):
                    for t in range(BT):
                        ins = pe.transpose(bank[:, c, t * P:(t + 1) * P], src[:, t, c * P:(c + 1) * P], ident[:])
                    ins.then_inc(made, 1)

            def wide(cen):
                return cen.unsqueeze(1).broadcast_to([P, D // E, E])

            def logits(b):
                pe.wait_ge(d_x2T, KC * (b + 1))
                need(pe, d_logit, 2 * b)
                for n in range(2):
                    for t in (2 * n, 2 * n + 1):
                        for c in range(KC):
                            at = slice(t * P, (t + 1) * P)
                            ins = split3(pe, bank[:, 4 + n, t % 2 * D:(t % 2 + 1) * D], x2T_hi[:, c, at], x2T_lo[:, c, at],
                                         wide(cen_hi[:, c, :]), wide(cen_lo[:, c, :]), c == 0, c == KC - 1)
                    ins.then_inc(pe_logit, 1)

            def batch(b, first, last):
                pe.wait_ge(ln1_done, BT * (b + 1))
                need(pe, d_pT, BT * b)
                transpose_rows(xn, pe_xT)
                pe.wait_ge(d_xT, KC * (b + 1))
                need(pe, d_o, BT * b)
                for m in range(KC):
                    for c in range(KC):
                        at = slice(m * P, (m + 1) * P)
                        ins = split3(pe, bank[:, 2 + m, :], a_hi[:, c, at], a_lo[:, c, at], xT_hi[:, c, :], xT_lo[:, c, :],
                                     c == 0, c == KC - 1)
                    ins.then_inc(pe_qT, 1)
                need(pe, d_logit, 2 * (b - 1)) if not first else None
                for n in range(2):
                    for t in (2 * n, 2 * n + 1):
                        for c in range(KC):
                            at = slice(t * P, (t + 1) * P)
                            ins = split3(pe, bank[:, 4 + n, t % 2 * D:(t % 2 + 1) * D], xT_hi[:, c, at], xT_lo[:, c, at],
                                         wv_hi[:, c, :], wv_lo[:, c, :], c == 0, c == KC - 1)
                    ins.then_inc(pe_v, 1)
                if not first:
                    pe.wait_ge(ln2_done, BT * b)
                    transpose_rows(x2, pe_x2T)

                def scores(i):
                    need(pe, a_exp, BT * b + max(i - 1, 0))
                    s = bank[:, 6 + i % 2, :]
                    n = max((i + 1) * P, 2 * P)
                    at = slice(i * P, (i + 1) * P)
                    for m in range(KC):
                        split3(pe, s[:, 0:n], qT_hi[:, m, at], qT_lo[:, m, at], xT_hi[:, m, 0:n], xT_lo[:, m, 0:n],
                               m == 0, False)
                    pe.matmul(s[:, at], ident_b[:], mask_b[:], start=False, stop=True).then_inc(pe_s, 1)

                def probsT(i):
                    pe.wait_ge(a_exp, BT * b + i + 1)
                    need(pe, d_pT, BT * b + i - 1) if i > 1 else None
                    for kb in range(i + 1):
                        at = slice(kb * P, (kb + 1) * P)
                        ins = pe.transpose(bank[:, i % 2, at], probs[:, i % 2, at], ident[:])
                    ins.then_inc(pe_pT, 1)

                def attend(i):
                    pe.wait_ge(d_pT, BT * b + i + 1)
                    need(pe, d_o, BT * b + i - 1) if i > 1 else None
                    for kb in range(i + 1):
                        at = slice(kb * P, (kb + 1) * P)
                        ins = split3(pe, bank[:, 2 + i % 2, 0:D], pT_hi[:, i % 2, at], pT_lo[:, i % 2, at],
                                     v_hi[:, kb, :], v_lo[:, kb, :], kb == 0, kb == i)
                    ins.then_inc(pe_o, 1)

                pe.wait_ge(d_qT, KC * (b + 1))
                scores(0)
                scores(1)
                pe.wait_ge(d_v, 2 * (b + 1))
                if not first:
                    logits(b - 1)
                probsT(0)
                scores(2)
                attend(0)
                probsT(1)
                scores(3)
                attend(1)
                probsT(2)
                attend(2)
                probsT(3)
                attend(3)

            over_batches(pe, batch)
            pe.wait_ge(ln2_done, BT * B)
            pe.wait_ge(d_pT, BT * B)
            transpose_rows(x2, pe_x2T)
            logits(B - 1)

            pe.wait_ge(hot_done, 2)
            pe.matmul(bank[:, 0, 0:(TILES + 1) * E], before_b[:], hot_b[:].rearrange("p t e -> p (t e)"), start=True, stop=False)
            for t in range(TILES):
                n = TILES - t
                ins = pe.matmul(bank[:, 0, (t + 1) * E:(TILES + 1) * E].rearrange("p (t e) -> p t e", e=E), ones_b[:],
                                hot_b[:, t:t + 1, :].broadcast_to([P, n, E]), start=False, stop=(t == TILES - 1))
            ins.then_inc(ranks, 1)

            def transpose_tile(q, k):
                J = RING * q + k
                pe.wait_ge(ld_t[k], 16 * (q + 1))
                need(pe, d_t, J - 1)
                for c in range(KC):
                    ins = pe.transpose(bank[:, k % 2, c * P:(c + 1) * P], ring[:, k, c * P:(c + 1) * P], ident[:])
                ins.then_inc(pe_t, 1)

            def weights_of(e, at):
                if isinstance(e, int):
                    return w_hi[:, e, at], w_lo[:, e, at]
                return w_hi[:, bass.ds(e, 1), at], w_lo[:, bass.ds(e, 1), at]

            def gate_up(q, k, e):
                J = RING * q + k
                pe.wait_ge(d_t, J + 1)
                need(pe, d_h, J - 1)
                for c in range(KC):
                    at = slice(c * P, (c + 1) * P)
                    rhi, rlo = weights_of(e, slice(c * 2 * I, (c + 1) * 2 * I))
                    ins = split3(pe, bank[:, 2 + k % 2, 0:2 * I], gT_hi[:, k % 2, at], gT_lo[:, k % 2, at], rhi, rlo,
                                 c == 0, c == KC - 1)
                ins.then_inc(pe_gu, 1)

            def hidden_T(q, k):
                J = RING * q + k
                pe.wait_ge(d_h, J + 1)
                need(pe, d_hT, J - 1)
                pe.transpose(bank[:, 4 + k % 2, 0:P], h[:, k % 2, :], ident[:]).then_inc(pe_hT, 1)

            def down(q, k, e):
                J = RING * q + k
                pe.wait_ge(d_hT, J + 1)
                need(pe, d_y, J - 1)
                rhi, rlo = weights_of(e, slice(KC * 2 * I, WE))
                split3(pe, bank[:, 6 + k % 2, 0:D], hT_hi[:, k % 2, :], hT_lo[:, k % 2, :], rhi, rlo, True, True)\
                    .then_inc(pe_y, 1)

            pe.wait_ge(w_split, 2 * (E + HALVES))
            pe.wait_ge(slots_done, 1)
            pipelined(pe, q_shared, SHARED_STEPS // RING,
                      [(1, transpose_tile), (0, lambda q, k: gate_up(q, k, E + k % 2)), (-1, hidden_T),
                       (-2, lambda q, k: down(q, k, E + k % 2))])

            pe.wait_ge(words_done, 1)
            held = {}

            def expert(q, k):
                key = str(q) if isinstance(q, int) else id(q)
                w = pe.value_load(word[0:1, bass.ds(q - q_routed, 1)]) if not isinstance(q, int) else \
                    pe.value_load(word[0:1, q - q_routed:q - q_routed + 1])
                return (w >> (ID_BITS * k)) & (E - 1)

            def routed_gate_up(q, k):
                held[k] = pe.snap(expert(q, k), min_val=0, max_val=E - 1)
                gate_up(q, k, held[k])

            def routed_down(q, k):
                down(q, k, pe.snap(expert(q, k), min_val=0, max_val=E - 1))

            pipelined(pe, q_routed, GROUPS,
                      [(1, transpose_tile), (0, routed_gate_up), (-1, hidden_T), (-2, routed_down)])


_INS = ['L0_attn_x', 'L0_attn_Wq', 'L0_attn_Wk', 'L0_attn_Wv', 'L0_ffn_centroids', 'L0_ffn_gate_bias', 'L0_ffn_wg_s',
        'L0_ffn_wu_s', 'L0_ffn_wd_s', 'L0_ffn_wg', 'L0_ffn_wu', 'L0_ffn_wd']
_OUTS = [((4, 512, 256), 'float32')]


def kernel(**inputs):
    import numpy as _np
    import concourse.bacc as _bacc
    from concourse import mybir as _mybir
    from concourse.bass_utils import run_bass_kernel_spmd as _run

    nc = _bacc.Bacc("TRN2", target_bir_lowering=False, num_devices=1)
    arrays, args = {}, []
    for name in _INS:
        a = _np.ascontiguousarray(inputs[name])
        arrays[f"in_{name}_dram"] = a
        args.append(nc.dram_tensor(f"in_{name}_dram", a.shape, _mybir.dt.from_np(a.dtype), kind="ExternalInput").ap())
    for i, (shape, dtype) in enumerate(_OUTS):
        dt = _mybir.dt.from_np(_np.dtype(dtype))
        args.append(nc.dram_tensor(f"out_{i}_dram", shape, dt, kind="ExternalOutput").ap())
    block_causal_attention_and_moe(nc, *args)
    r = _run(nc, [arrays], core_ids=[0])
    got = tuple(r.results[0][f"out_{i}_dram"] for i in range(len(_OUTS)))
    return got[0]
```

```python
from contextlib import ExitStack

import concourse.bass as bass
from concourse import mybir

P = 128
ALU = mybir.AluOpType
ACT = mybir.ActivationFunctionType
AX = mybir.AxisListType.X
F32 = mybir.dt.float32
F32R = mybir.dt.float32r
BF16 = mybir.dt.bfloat16
U32 = mybir.dt.uint32
I32 = mybir.dt.int32

LEAST_LOGIT = -87.0
LN_EPS = 1e-5
GATE_EPS = 1e-9
SHARED_RATIO = 0.1
MASKED = -1e30

RING = 8
ID_BITS = 4
IDS = 4


def block_causal_attention_and_moe(
    nc: bass.Bass, x, Wq, Wk, Wv, centroids, gate_bias, wg_s, wu_s, wd_s, wg, wu, wd, out
):
    B, S, D = x.shape
    E, _, I = wg.shape
    TILES = B * S // P
    BT = S // P
    KC = D // P
    HALVES = wg_s.shape[1] // I
    assert D == 256 and I == P and BT == 4 and E == 16 and HALVES == 2
    SCALE = float(D) ** -0.5
    SHARED_STEPS = TILES * HALVES
    EXPERT_TILES = 2 * TILES + E
    GROUPS = EXPERT_TILES // RING
    WORDS = EXPERT_TILES // IDS
    SLOTS = EXPERT_TILES * P
    ROW = D + 2
    WE = KC * 2 * I + D
    RESULTS = 2 * TILES * P

    expert_rows = nc.dram_tensor("expert_rows", (SLOTS, ROW), F32, kind="Internal").ap()
    expert_out = nc.dram_tensor("expert_out", (RESULTS, D), F32, kind="Internal").ap()

    ctx = ExitStack()
    with ctx:
        def sb(name, shape, dt=F32):
            return ctx.enter_context(nc.sbuf_tensor(name, shape, dt))

        def sem(name):
            return ctx.enter_context(nc.semaphore(name))

        res = sb("res", [P, TILES, D])
        rows2 = sb("rows2", [P, TILES, ROW])
        before = rows2[:].rearrange("p t r -> p (t r)")
        wqk_raw = before[:, 0:2 * KC * D].rearrange("p (w c n) -> p w c n", w=2, c=KC)
        wv_raw = before[:, 2 * KC * D:3 * KC * D].rearrange("p (c n) -> p c n", c=KC)
        cen_raw = before[0:E, 3 * KC * D:3 * KC * D + D]
        both = before[:, 0:2 * BT * 2 * D].rearrange("p (s t c d) -> p s t c d", s=2, t=BT, c=2)
        w_hi = sb("w_hi", [P, E + HALVES, WE], F32R)
        w_lo = sb("w_lo", [P, E + HALVES, WE], F32R)
        w_raw = sb("w_raw", [P, 2, WE])
        ident = sb("ident", [P, P])
        ident_b = sb("ident_b", [P, P], BF16)
        mask_b = sb("mask_b", [P, P], BF16)
        before_b = sb("before_b", [P, P], BF16)
        ones_b = sb("ones_b", [P, P], BF16)
        template = sb("template", [P, ROW])
        a_hi = sb("a_hi", [P, KC, D], F32R)
        a_lo = sb("a_lo", [P, KC, D], F32R)
        wv_hi = sb("wv_hi", [P, KC, D], F32R)
        wv_lo = sb("wv_lo", [P, KC, D], F32R)
        cen_hi = sb("cen_hi", [P, KC, E], F32R)
        cen_lo = sb("cen_lo", [P, KC, E], F32R)
        stats = sb("stats", [P, 2, BT, 6])
        mv = sb("mv", [P, 2, BT, 2])
        veps = sb("veps", [P, 2, BT])
        rstd = sb("rstd", [P, 2, BT])
        minus_half = sb("minus_half", [P, BT])
        smax = sb("smax", [P, BT])
        nbias = sb("nbias", [P, BT])
        rsum = sb("rsum", [P, BT])
        rinv = sb("rinv", [P, BT])
        en = sb("en", [P, TILES, E])
        logit = sb("logit", [P, BT, E])
        bias_all = sb("bias_all", [P, E])
        row0 = sb("row0", [P, TILES], U32)
        iota_u = sb("iota_u", [P, EXPERT_TILES], I32)
        ones_e = sb("ones_e", [P, E])
        weight = sb("weight", [P, 2, TILES])

        with ExitStack() as attention:
            def asb(name, shape, dt=F32):
                return attention.enter_context(nc.sbuf_tensor(name, shape, dt))

            xn = asb("xn", [P, BT, D])
            x2 = asb("x2", [P, BT, D])
            probs = asb("probs", [P, 2, S])
            wqkT = x2[:].rearrange("p (w c) n -> p w c n", w=2)
            xT_hi = asb("xT_hi", [P, KC, S], F32R)
            xT_lo = asb("xT_lo", [P, KC, S], F32R)
            qT_hi = asb("qT_hi", [P, KC, S], F32R)
            qT_lo = asb("qT_lo", [P, KC, S], F32R)
            v_hi = asb("v_hi", [P, BT, D], F32R)
            v_lo = asb("v_lo", [P, BT, D], F32R)
            pT_hi = asb("pT_hi", [P, 2, S], F32R)
            pT_lo = asb("pT_lo", [P, 2, S], F32R)
            x2T_hi, x2T_lo = pT_hi, pT_lo

        aff = sb("aff", [P, TILES, E])
        biased = sb("biased", [P, TILES, E])
        top8 = sb("top8", [P, TILES, 8])
        top8_at = sb("top8_at", [P, TILES, 8], U32)
        top_at = sb("top_at", [P, TILES, 2])
        iota_f = sb("iota_f", [P, EXPERT_TILES])
        hot = sb("hot", [P, 2, TILES, E])
        picked = sb("picked", [P, TILES, E])
        hot_b = sb("hot_b", [P, TILES + 1, E], BF16)
        taff = sb("taff", [P, 2, TILES])
        tsum = sb("tsum", [P, TILES])
        pos = sb("pos", [P, TILES, E])
        slot_f = sb("slot_f", [P, 2, TILES])
        slot_u = sb("slot_u", [P, 2, TILES], U32)
        cnt = sb("cnt", [P, E])
        cnt_i = sb("cnt_i", [P, E], I32)
        tiles_f = sb("tiles_f", [P, E])
        ends = sb("ends", [P, E])
        base = sb("base", [P, E])
        past = sb("past", [1, EXPERT_TILES, E])
        tile_expert = sb("tile_expert", [1, EXPERT_TILES])
        digit = sb("digit", [1, IDS])
        shifted = sb("shifted", [1, WORDS, IDS])
        word_f = sb("word_f", [1, WORDS])
        word = sb("word", [1, WORDS], U32)
        ring = sb("ring", [P, RING, ROW])
        dest = sb("dest", [P, RING], U32)
        gate = sb("gate", [P, RING])
        gT_hi = sb("gT_hi", [P, 2, D], F32R)
        gT_lo = sb("gT_lo", [P, 2, D], F32R)
        sg = sb("sg", [P, 2, I])
        h = sb("h", [P, 2, I])
        hT_hi = sb("hT_hi", [P, 2, P], F32R)
        hT_lo = sb("hT_lo", [P, 2, P], F32R)
        y_sb = sb("y_sb", [P, RING, D])

        bank = ctx.enter_context(nc.psum_tensor("bank", [P, 8, 512], F32))

        ld_wqk = sem("ld_wqk"); ld_wv = sem("ld_wv"); ld_cen = sem("ld_cen"); ld_bias = sem("ld_bias")
        ld_x = [sem(f"ld_x{b}") for b in range(B)]
        ld_w = [sem(f"ld_w{k}") for k in range(2)]
        filled = sem("filled")
        c_step = sem("c_step")
        consts = sem("consts")
        const_b = sem("const_b")
        w_hi_done = sem("w_hi_done"); w_lo_done = sem("w_lo_done")
        wT_done = sem("wT_done"); wT_copied = sem("wT_copied"); a_done = sem("a_done")
        a_hi_done = sem("a_hi_done"); a_lo_done = sem("a_lo_done"); wv_done = sem("wv_done")
        cenT = sem("cenT"); cen_hi_done = sem("cen_hi_done"); cen_done = sem("cen_done")
        ln1_stats = sem("ln1_stats"); ln1_mv = sem("ln1_mv"); ln1_ve = sem("ln1_ve"); ln1_rstd = sem("ln1_rstd")
        ln1_done = sem("ln1_done")
        ln2_stats = sem("ln2_stats"); ln2_mv = sem("ln2_mv"); ln2_ve = sem("ln2_ve"); ln2_rstd = sem("ln2_rstd")
        ln2_done = sem("ln2_done"); rows_done = sem("rows_done")
        pe_xT = sem("pe_xT"); a_xT = sem("a_xT"); d_xT = sem("d_xT")
        pe_qT = sem("pe_qT"); a_qT = sem("a_qT"); d_qT = sem("d_qT")
        pe_v = sem("pe_v"); a_v = sem("a_v"); d_v = sem("d_v")
        pe_s = sem("pe_s"); d_max = sem("d_max"); d_nbias = sem("d_nbias"); a_exp = sem("a_exp")
        pe_pT = sem("pe_pT"); a_pT = sem("a_pT"); d_pT = sem("d_pT")
        pe_o = sem("pe_o"); d_rinv = sem("d_rinv"); d_o = sem("d_o")
        pe_x2T = sem("pe_x2T"); a_x2T = sem("a_x2T"); d_x2T = sem("d_x2T")
        pe_logit = sem("pe_logit"); d_logit = sem("d_logit"); a_en = sem("a_en")
        apart = sem("apart")
        r_step = sem("r_step")
        hot_done = sem("hot_done"); ranks = sem("ranks"); slots_done = sem("slots_done"); words_done = sem("words_done")
        first_cols = sem("first_cols"); second_cols = sem("second_cols"); sent = [sem("sent0"), sem("sent1")]
        ld_t = [sem(f"ld_t{k}") for k in range(RING)]
        pe_t = sem("pe_t"); a_t = sem("a_t"); d_t = sem("d_t"); d_dest = sem("d_dest")
        pe_gu = sem("pe_gu"); a_silu = sem("a_silu"); d_h = sem("d_h")
        pe_hT = sem("pe_hT"); a_hT = sem("a_hT"); d_hT = sem("d_hT")
        pe_y = sem("pe_y"); d_y = sem("d_y")
        sc_y = [sem(f"sc_y{k}") for k in range(RING)]
        ld_both = [sem(f"ld_both{k}") for k in range(2)]
        f_part = sem("f_part"); f_done = sem("f_done")
        stored = sem("stored")

        x_v = x.rearrange("b (t p) d -> b p t d", p=P)
        out_v = out.rearrange("b (t p) d -> b p t d", p=P)
        both_v = expert_out.rearrange("(b t p c) d -> b p t c d", b=B, p=P, c=2)

        def need(eng, s, v):
            if not isinstance(v, int) or v > 0:
                eng.wait_ge(s, v)

        def wait_apart(eng, s, v):
            eng.wait_ge(s, v)
            if not isinstance(v, int):
                eng.sem_inc(apart, 1)

        def over_batches(eng, body, after=None):
            body(0, first=True, last=False)
            with eng.Fori(1, B - 1) as b:
                body(b, first=False, last=False)
            body(B - 1, first=False, last=True)

        position = [0]

        def pipelined(eng, q0, groups, stages, begin=None):
            n = RING * groups

            def group(q, first, last, extra=0):
                if begin:
                    begin(q)
                for k in range(RING + extra):
                    for lag, f in stages:
                        kk = k + lag
                        if first and kk < 0:
                            continue
                        if last and kk >= RING:
                            continue
                        if last and k >= RING and kk < 0:
                            continue
                        position[0] = kk
                        f(q + kk // RING, kk % RING)

            for lag, f in stages:
                for k in range(max(lag, 0)):
                    f(q0 + k // RING, k % RING)
            group(q0, True, False)
            with eng.Fori(q0 + 1, q0 + groups - 1) as q:
                group(q, False, False)
            group(q0 + groups - 1, False, True, extra=2)

        q_shared, q_routed = 0, SHARED_STEPS // RING

        def split3(pe, acc, hi, lo, rhi, rlo, first, last):
            pe.matmul(acc, lo, rhi, start=first, stop=False)
            pe.matmul(acc, hi, rlo, start=False, stop=False)
            return pe.matmul(acc, hi, rhi, start=False, stop=last)

        block = ctx.enter_context(nc.Block())

        @block.sync
        def _(sp):
            sp.dma_start(res[:, 0:BT, :], x_v[0]).then_inc(ld_x[0], 16)
            for n, w in enumerate((Wq, Wk)):
                sp.dma_start(wqk_raw[:, n], w.rearrange("(c p) n -> p c n", p=P)).then_inc(ld_wqk, 16)
            sp.dma_start(wv_raw, Wv.rearrange("(c p) n -> p c n", p=P)).then_inc(ld_wv, 16)
            sp.dma_start(cen_raw, centroids).then_inc(ld_cen, 16)

            def gate_up(k, half):
                return w_raw[:, k, 0:KC * 2 * I].rearrange("p (c n) -> p c n", c=KC)[:, :, half * I:(half + 1) * I]

            for k in range(HALVES):
                for half, w in enumerate((wg_s, wu_s)):
                    sp.dma_start(gate_up(k, half), w[:, k * I:(k + 1) * I].rearrange("(c p) i -> p c i", p=P)).then_inc(ld_w[k], 16)
                sp.dma_start(w_raw[:, k, KC * 2 * I:WE], wd_s[k * I:(k + 1) * I, :]).then_inc(ld_w[k], 16)
            for b in range(1, B):
                sp.dma_start(res[:, b * BT:(b + 1) * BT, :], x_v[b]).then_inc(ld_x[b], 16)
            sp.dma_start(bias_all[:], gate_bias.rearrange("(a e) -> a e", a=1).broadcast_to([P, E])).then_inc(ld_bias, 16)

            sp.wait_ge(consts, 1)
            sp.dma_start(expert_rows.rearrange("(j p) r -> p j r", p=P),
                         template[:].unsqueeze(1).broadcast_to([P, EXPERT_TILES, ROW])).then_inc(filled, 16)

            with sp.Fori(0, E // 2) as m:
                for k in range(2):
                    e = 2 * m + k
                    sp.wait_ge(w_lo_done, e + HALVES - 1)
                    for half, w in enumerate((wg, wu)):
                        sp.dma_start(gate_up(k, half), w[bass.ds(e, 1)].rearrange("a (c p) i -> p (a c) i", p=P)).then_inc(ld_w[k], 16)
                    sp.dma_start(w_raw[:, k, KC * 2 * I:WE], wd[bass.ds(e, 1)].rearrange("a p d -> p (a d)")).then_inc(ld_w[k], 16)

            def load_shared(q, k):
                need(sp, pe_t, RING * (q - 1) + k + 1)
                sp.dma_start(ring[:, k, 0:D], rows2[:, bass.ds(RING // HALVES * q + k // HALVES, 1), 0:D]).then_inc(ld_t[k], 16)

            sp.wait_ge(rows_done, B)
            for k in range(RING):
                load_shared(0, k)
            with sp.Fori(1, q_routed) as q:
                for k in range(RING):
                    load_shared(q, k)

            def load_routed(q, k):
                if not isinstance(q, int):
                    wait_apart(sp, d_dest, 2 * (RING * (q - 1 - q_routed) + k + 1))
                wait_apart(sp, pe_t, RING * (q - 1) + k + 1)
                sp.dma_start(ring[:, k, :], expert_rows[bass.ds((RING * (q - q_routed) + k) * P, P), :]).then_inc(ld_t[k], 16)

            for s in sent:
                sp.wait_ge(s, 16 * TILES)
            for k in range(RING):
                load_routed(q_routed, k)
            with sp.Fori(q_routed + 1, q_routed + GROUPS) as q:
                for k in range(RING):
                    load_routed(q, k)

            for k in range(RING):
                sp.wait_ge(sc_y[k], 16 * GROUPS)
            for b in range(B):
                if b >= 2:
                    sp.wait_ge(f_done, b - 1)
                sp.dma_start(both[:, b % 2], both_v[b]).then_inc(ld_both[b % 2], 16)
                if b >= 2:
                    sp.dma_start(out_v[b - 2], res[:, (b - 2) * BT:(b - 1) * BT, :]).then_inc(stored, 16)
            for b in range(B - 2, B):
                sp.wait_ge(f_done, b + 1)
                sp.dma_start(out_v[b], res[:, b * BT:(b + 1) * BT, :]).then_inc(stored, 16)
            sp.wait_ge(stored, 16 * B)

        @block.gpsimd
        def _(pool):
            g = nc.gpsimd
            done = [0]

            def step(ins):
                done[0] += 1
                ins.then_inc(c_step, 1)
                pool.wait_ge(c_step, done[0])

            step(g.memset(ident[:], 0.0))
            step(g.affine_select(out=ident[:], in_=ident[:], compare_op=ALU.not_equal, fill=1.0, base=0,
                                 pattern=[[-1, P]], channel_multiplier=1))
            step(g.memset(minus_half[:], -0.5))
            step(g.memset(mask_b[:], 0.0))
            step(g.affine_select(out=mask_b[:], in_=mask_b[:], compare_op=ALU.is_ge, fill=MASKED, base=0,
                                 pattern=[[-1, P]], channel_multiplier=1))
            step(g.memset(before_b[:], 1.0))
            step(g.affine_select(out=before_b[:], in_=before_b[:], compare_op=ALU.is_gt, fill=0.0, base=0,
                                 pattern=[[1, P]], channel_multiplier=-1))
            step(g.memset(ones_b[:], 1.0))
            step(g.memset(template[:], 0.0))
            step(g.iota(template[:, D:D + 1].bitcast(U32), pattern=[[0, 1]], base=RESULTS, channel_multiplier=1))
            step(g.iota(row0[:], pattern=[[2 * P, TILES]], base=0, channel_multiplier=2))
            step(g.iota(iota_u[:], pattern=[[1, EXPERT_TILES]], base=0, channel_multiplier=0))
            step(g.tensor_copy(ident_b[:], ident[:]))
            g.memset(ones_e[:], 1.0).then_inc(consts, 1)

            def rsqrt(n, b, mv_ready, added, ready):
                wait_apart(pool, mv_ready, b + 1)
                g.tensor_scalar(veps[:, n, :], mv[:, n, :, 1], LN_EPS, None, ALU.add).then_inc(added, 1)
                pool.wait_ge(added, b + 1)
                g.tensor_tensor(rstd[:, n, :], veps[:, n, :], minus_half[:], ALU.pow).then_inc(ready, 1)

            def weights_lo(s, e, k):
                wait_apart(pool, w_hi_done, s + 1)
                g.tensor_tensor(w_lo[:, bass.ds(e, 1), :], w_raw[:, k:k + 1, :], w_hi[:, bass.ds(e, 1), :].bitcast(F32),
                                ALU.subtract).then_inc(w_lo_done, 1)

            def rows_of(b):
                wait_apart(pool, ln2_done, BT * (b + 1))
                g.tensor_copy(rows2[:, bass.ds(BT * b, BT), 0:D], x2[:]).then_inc(rows_done, 1)

            rsqrt(0, 0, ln1_mv, ln1_ve, ln1_rstd)
            for n in range(HALVES):
                weights_lo(n, E + n, n)

            def batch(b, first, last):
                if not first:
                    rows_of(b - 1)
                for n in range(2):
                    weights_lo(HALVES + BT * b + n, BT * b + n, n)
                if not last:
                    rsqrt(0, b + 1, ln1_mv, ln1_ve, ln1_rstd)
                for n in range(2):
                    weights_lo(HALVES + BT * b + 2 + n, BT * b + 2 + n, n)
                rsqrt(1, b, ln2_mv, ln2_ve, ln2_rstd)

            over_batches(pool, batch)
            rows_of(B - 1)

            pool.wait_ge(filled, 16)
            pool.wait_ge(slots_done, 1)
            pool.wait_ge(first_cols, 2)
            for c in range(2):
                if c:
                    pool.wait_ge(sent[0], 16 * TILES)
                    g.tensor_scalar(rows2[:, :, D].bitcast(U32), rows2[:, :, D].bitcast(U32), 1.0, None, ALU.add).then_inc(second_cols, 1)
                    g.tensor_copy(rows2[:, :, D + 1], weight[:, 1]).then_inc(second_cols, 1)
                    pool.wait_ge(second_cols, 2)
                for t in range(TILES):
                    g.indirect_dma_start(expert_rows, bass.IndirectOffsetOnAxis(slot_u[:, c, t:t + 1], 0),
                                         rows2[:, t, :], None).then_inc(sent[c], 16)

            def scatter_results(q, k):
                wait_apart(pool, d_y, RING * q + k + 1)
                g.indirect_dma_start(expert_out, bass.IndirectOffsetOnAxis(dest[:, k:k + 1], 0),
                                     y_sb[:, k, :], None, bounds_check=RESULTS - 1, oob_is_err=False).then_inc(sc_y[k], 16)

            with pool.Fori(q_routed, q_routed + GROUPS) as q:
                for k in range(RING):
                    scatter_results(q, k)

        @block.scalar
        def _(act):
            a = nc.scalar
            def weights_hi(s, e, k, nth):
                act.wait_ge(ld_w[k], 48 * (nth + 1))
                a.activation(w_hi[:, bass.ds(e, 1), :], w_raw[:, k:k + 1, :], ACT.Copy).then_inc(w_hi_done, 1)

            act.wait_ge(ld_wv, 16)
            a.activation(wv_hi[:], wv_raw, ACT.Copy).then_inc(wv_done, 1)
            for n in range(2):
                act.wait_ge(wT_done, n + 1)
                a.activation(wqkT[:, n].rearrange("p c n -> p (c n)"), bank[:, n, :], ACT.Copy).then_inc(wT_copied, 1)
            act.wait_ge(a_done, 1)
            a.activation(a_hi[:].rearrange("p c n -> p (c n)"), bank[:, 2, :], ACT.Copy).then_inc(a_hi_done, 1)
            act.wait_ge(cenT, 1)
            a.activation(cen_hi[:], bank[:, 3, 0:KC * E].rearrange("p (c e) -> p c e", c=KC),
                         ACT.Copy).then_inc(cen_hi_done, 1)

            def transposed(b, made, mine, hi, freed, freed_at):
                need(act, freed, freed_at)
                for c in range(KC):
                    act.wait_ge(made, KC * b + c + 1)
                    a.activation(hi[:, c, :], bank[:, 4 + c, :], ACT.Copy).then_inc(mine, 1)

            def gates(b):
                act.wait_ge(d_logit, 2 * (b + 1))
                a.activation(en[:, bass.ds(BT * b, BT), :], logit[:],
                             ACT.Exp, scale=-1.0).then_inc(a_en, 1)

            def batch(b, first, last):
                need(act, pe_o, BT * b)
                for n in range(2):
                    act.wait_ge(pe_v, 2 * b + n + 1)
                    a.activation(v_hi[:, 2 * n:2 * n + 2, :].rearrange("p t d -> p (t d)"), bank[:, n, :],
                                 ACT.Copy).then_inc(a_v, 1)
                for m in range(KC):
                    act.wait_ge(pe_qT, KC * b + m + 1)
                    a.activation(qT_hi[:, m, :], bank[:, 2 + m, :], ACT.Copy).then_inc(a_qT, 1)
                if not first:
                    transposed(b - 1, pe_x2T, a_x2T, x2T_hi, pe_o, BT * b)
                weights_hi(HALVES + BT * b, BT * b, 0, 2 * b + 1)

                def exps(n):
                    i, cols = BT - 1 - n, (BT - n) * P
                    act.wait_ge(d_nbias, BT * b + n + 1)
                    need(act, pe_pT, BT * b + max(n - 1, 0))
                    a.activation(probs[:, n % 2, 0:cols], bank[:, 6 + n % 2, 0:cols], ACT.Exp, bias=nbias[:, i:i + 1],
                                 scale=SCALE, accum_out=rsum[:, i:i + 1]).then_inc(a_exp, 1)

                def probsT(n):
                    cols = (BT - n) * P
                    act.wait_ge(pe_pT, BT * b + n + 1)
                    need(act, pe_o, BT * b + max(n - 1, 0))
                    a.activation(pT_hi[:, n % 2, 0:cols], bank[:, n % 2, 0:cols], ACT.Copy).then_inc(a_pT, 1)

                exps(0)
                exps(1)
                weights_hi(HALVES + BT * b + 1, BT * b + 1, 1, 2 * b + 1)
                probsT(0)
                exps(2)
                if not first:
                    gates(b - 1)
                probsT(1)
                exps(3)
                weights_hi(HALVES + BT * b + 2, BT * b + 2, 0, 2 * b + 2)
                probsT(2)
                if not last:
                    transposed(b + 1, pe_xT, a_xT, xT_hi, pe_s, BT * (b + 1))
                probsT(3)
                weights_hi(HALVES + BT * b + 3, BT * b + 3, 1, 2 * b + 2)

            transposed(0, pe_xT, a_xT, xT_hi, None, 0)
            for n in range(HALVES):
                weights_hi(n, E + n, n, 0)
            over_batches(act, batch)
            transposed(B - 1, pe_x2T, a_x2T, x2T_hi, pe_o, BT * B)
            gates(B - 1)

            def tile_hi(q, k):
                J = RING * q + k
                act.wait_ge(pe_t, J + 1)
                need(act, pe_gu, J - 1)
                a.activation(gT_hi[:, k % 2, :], bank[:, k % 2, 0:D], ACT.Copy).then_inc(a_t, 1)

            def silu(q, k):
                J = RING * q + k
                act.wait_ge(pe_gu, J + 1)
                need(act, d_h, J - 1)
                a.activation(sg[:, k % 2, :], bank[:, 2 + k % 2, 0:I], ACT.Silu).then_inc(a_silu, 1)

            def hidden_hi(q, k):
                J = RING * q + k
                act.wait_ge(pe_hT, J + 1)
                need(act, pe_y, J - 1)
                a.activation(hT_hi[:, k % 2, :], bank[:, 4 + k % 2, 0:P], ACT.Copy).then_inc(a_hT, 1)

            stages = [(1, tile_hi), (0, silu), (-1, hidden_hi)]
            pipelined(act, q_shared, SHARED_STEPS // RING, stages)
            pipelined(act, q_routed, GROUPS, stages)

        @block.vector
        def _(dve):
            v = nc.vector

            def res_tile(b, t):
                return res[:, bass.ds(BT * b + t, 1), :].rearrange("p a d -> p (a d)") if not isinstance(b, int) \
                    else res[:, BT * b + t, :]

            def tile_stats(n, b, t, stat):
                return v.bn_stats(stats[:, n, t, :], res_tile(b, t)).then_inc(stat, 1)

            def batch_stats(n, b, stat, mvs):
                wait_apart(dve, stat, BT * (b + 1))
                for t in range(BT):
                    ins = v.bn_aggr(mv[:, n, t, :], stats[:, n, t, :])
                ins.then_inc(mvs, 1)

            def normalized(n, b, dst, ready, done, dst_free, free_at):
                dve.wait_ge(ready, b + 1)
                need(dve, dst_free, free_at)
                for t in range(BT):
                    v.tensor_scalar(dst[:, t, :], res_tile(b, t), mv[:, n, t, 0:1], rstd[:, n, t:t + 1],
                                    ALU.subtract, ALU.mult).then_inc(done, 1)

            def sub(dst, src, hi):
                return v.tensor_tensor(dst, src, hi.bitcast(F32), ALU.subtract)

            def transposed(b, his, mine, lo, hi, freed, freed_at):
                need(dve, freed, freed_at)
                for c in range(KC):
                    dve.wait_ge(his, KC * b + c + 1)
                    sub(lo[:, c, :], bank[:, 4 + c, :], hi[:, c, :]).then_inc(mine, 1)

            dve.wait_ge(ld_x[0], 16)
            for t in range(BT):
                tile_stats(0, 0, t, ln1_stats)
            batch_stats(0, 0, ln1_stats, ln1_mv)
            normalized(0, 0, xn, ln1_rstd, ln1_done, None, 0)
            dve.wait_ge(wv_done, 1)
            sub(wv_lo[:], wv_raw, wv_hi[:]).then_inc(wv_done, 1)
            dve.wait_ge(a_hi_done, 1)
            sub(a_lo[:].rearrange("p c n -> p (c n)"), bank[:, 2, :], a_hi[:].rearrange("p c n -> p (c n)")).then_inc(a_lo_done, 1)
            dve.wait_ge(cen_hi_done, 1)
            sub(cen_lo[:], bank[:, 3, 0:KC * E].rearrange("p (c e) -> p c e", c=KC), cen_hi[:]).then_inc(cen_done, 1)
            transposed(0, a_xT, d_xT, xT_lo, xT_hi, None, 0)

            def clamped(b):
                for n in range(2):
                    dve.wait_ge(pe_logit, 2 * b + n + 1)
                    v.tensor_scalar(logit[:, 2 * n:2 * n + 2, :],
                                    bank[:, 4 + n, :].rearrange("p (t n) -> p t n", t=2)[:, :, 0:E],
                                    LEAST_LOGIT, None, ALU.max).then_inc(d_logit, 1)

            def batch(b, first, last):
                need(dve, pe_o, BT * b)
                for n in range(2):
                    dve.wait_ge(a_v, 2 * b + n + 1)
                    sub(v_lo[:, 2 * n:2 * n + 2, :].rearrange("p t d -> p (t d)"), bank[:, n, :],
                        v_hi[:, 2 * n:2 * n + 2, :].rearrange("p t d -> p (t d)")).then_inc(d_v, 1)
                if not first:
                    normalized(1, b - 1, x2, ln2_rstd, ln2_done, None, 0)
                for m in range(KC):
                    dve.wait_ge(a_qT, KC * b + m + 1)
                    sub(qT_lo[:, m, :], bank[:, 2 + m, :], qT_hi[:, m, :]).then_inc(d_qT, 1)
                if not first:
                    transposed(b - 1, a_x2T, d_x2T, x2T_lo, x2T_hi, pe_o, BT * b)
                if not last:
                    if first:
                        dve.wait_ge(ld_x[1], 16)
                    else:
                        for n in range(2, B):
                            dve.wait_ge(ld_x[n], 16)
                    for t in range(BT):
                        tile_stats(0, b + 1, t, ln1_stats)
                    batch_stats(0, b + 1, ln1_stats, ln1_mv)

                def row_max(n):
                    i = BT - 1 - n
                    dve.wait_ge(pe_s, BT * b + n + 1)
                    v.reduce_max(smax[:, i:i + 1], bank[:, 6 + n % 2, 0:(i + 1) * P], AX).then_inc(d_max, 1)
                    dve.wait_ge(d_max, BT * b + n + 1)
                    v.tensor_scalar(nbias[:, i:i + 1], smax[:, i:i + 1], -SCALE, None, ALU.mult).then_inc(d_nbias, 1)

                def probsT(n):
                    cols = (BT - n) * P
                    dve.wait_ge(a_pT, BT * b + n + 1)
                    need(dve, pe_o, BT * b + max(n - 1, 0))
                    sub(pT_lo[:, n % 2, 0:cols], bank[:, n % 2, 0:cols], pT_hi[:, n % 2, 0:cols]).then_inc(d_pT, 1)

                def attended(n):
                    i = BT - 1 - n
                    dve.wait_ge(a_exp, BT * b + n + 1)
                    v.reciprocal(rinv[:, i:i + 1], rsum[:, i:i + 1]).then_inc(d_rinv, 1)
                    dve.wait_ge(d_rinv, BT * b + n + 1)
                    dve.wait_ge(pe_o, BT * b + n + 1)
                    r = res_tile(b, i)
                    v.scalar_tensor_tensor(out=r, in0=bank[:, 2 + n % 2, 0:D], scalar=rinv[:, i:i + 1], in1=r,
                                           op0=ALU.mult, op1=ALU.add).then_inc(d_o, 1)

                def attended_stats(n):
                    wait_apart(dve, d_o, BT * b + n + 1)
                    tile_stats(1, b, BT - 1 - n, ln2_stats)

                row_max(0)
                row_max(1)
                if not first:
                    clamped(b - 1)
                probsT(0)
                row_max(2)
                if not last:
                    normalized(0, b + 1, xn, ln1_rstd, ln1_done, pe_xT, KC * (b + 1))
                attended(0)
                probsT(1)
                row_max(3)
                attended_stats(0)
                attended(1)
                probsT(2)
                attended_stats(1)
                if not last:
                    transposed(b + 1, a_xT, d_xT, xT_lo, xT_hi, pe_s, BT * (b + 1))
                attended(2)
                probsT(3)
                attended_stats(2)
                attended(3)
                attended_stats(3)
                batch_stats(1, b, ln2_stats, ln2_mv)

            over_batches(dve, batch)
            normalized(1, B - 1, x2, ln2_rstd, ln2_done, None, 0)
            transposed(B - 1, a_x2T, d_x2T, x2T_lo, x2T_hi, pe_o, BT * B)
            clamped(B - 1)

            n_step = [0]

            def step(ins):
                n_step[0] += 1
                ins.then_inc(r_step, 1)
                dve.wait_ge(r_step, n_step[0])

            def over_e(ap):
                return ap.unsqueeze(2).broadcast_to([P, TILES, E])

            def over_t(ap):
                return ap.unsqueeze(1).broadcast_to([P, TILES, E])

            dve.wait_ge(a_en, B)
            dve.wait_ge(rows_done, B)
            dve.wait_ge(ld_bias, 16)
            step(v.tensor_scalar(en[:], en[:], 1.0, None, ALU.add))
            step(v.reciprocal(aff[:], en[:]))
            step(v.tensor_tensor(biased[:], aff[:], over_t(bias_all[:]), ALU.add))
            for t in range(TILES):
                ins = v.max(top8[:, t, :], biased[:, t, :])
            step(ins)
            for t in range(TILES):
                ins = v.max_index(top8_at[:, t, :], top8[:, t, :], biased[:, t, :])
            step(ins)
            v.tensor_copy(iota_f[:], iota_u[:])
            step(v.tensor_copy(top_at[:], top8_at[:, :, 0:2]))
            for c in range(2):
                ins = v.tensor_tensor(hot[:, c], over_t(iota_f[:, 0:E]), over_e(top_at[:, :, c]), ALU.is_equal)
            step(ins)
            v.memset(hot_b[:, TILES, :], 0.0).then_inc(hot_done, 1)
            v.tensor_tensor(hot_b[:, 0:TILES, :], hot[:, 0], hot[:, 1], ALU.add).then_inc(hot_done, 1)
            for c in range(2):
                step(v.tensor_tensor(picked[:], hot[:, c], aff[:], ALU.mult))
                step(v.tensor_reduce(taff[:, c], picked[:], AX, ALU.add))
            dve.wait_ge(ranks, 1)
            step(v.tensor_scalar(cnt[:], bank[:, 7, TILES * E:(TILES + 1) * E], float(P - 1), None, ALU.add))
            step(v.tensor_copy(cnt_i[:], cnt[:]))
            step(v.tensor_scalar(cnt_i[:], cnt_i[:], P.bit_length() - 1, None, ALU.arith_shift_right))
            step(v.tensor_copy(tiles_f[:], cnt_i[:]))
            step(v.tensor_tensor_scan(ends[:], ones_e[:], tiles_f[:], 0.0, ALU.mult, ALU.add))
            step(v.tensor_tensor(base[:], ends[:], tiles_f[:], ALU.subtract))
            step(v.tensor_scalar(base[:], base[:], float(P), None, ALU.mult))
            step(v.tensor_tensor(pos[:], bank[:, 7, 0:TILES * E].rearrange("p (t e) -> p t e", t=TILES),
                                 over_t(base[:]), ALU.add))
            for c in range(2):
                step(v.tensor_tensor(picked[:], hot[:, c], pos[:], ALU.mult))
                step(v.tensor_reduce(slot_f[:, c], picked[:], AX, ALU.add))
            v.tensor_copy(slot_u[:], slot_f[:]).then_inc(slots_done, 1)
            step(v.tensor_tensor(tsum[:], taff[:, 0], taff[:, 1], ALU.add))
            step(v.tensor_scalar(tsum[:], tsum[:], GATE_EPS, None, ALU.add))
            step(v.reciprocal(tsum[:], tsum[:]))
            for c in range(2):
                ins = v.tensor_tensor(weight[:, c], taff[:, c], tsum[:], ALU.mult)
            step(ins)
            dve.wait_ge(rows_done, B)
            v.tensor_copy(rows2[:, :, D + 1], weight[:, 0]).then_inc(first_cols, 1)
            v.tensor_copy(rows2[:, :, D].bitcast(U32), row0[:]).then_inc(first_cols, 1)
            step(v.tensor_tensor(past[:], ends[0:1, :].unsqueeze(1).broadcast_to([1, EXPERT_TILES, E]),
                                 iota_f[0:1, :].unsqueeze(2).broadcast_to([1, EXPERT_TILES, E]), ALU.is_le))
            step(v.tensor_reduce(tile_expert[:], past[:], AX, ALU.add))
            step(v.tensor_scalar(tile_expert[:], tile_expert[:], float(E - 1), None, ALU.min))
            for k in range(IDS):
                ins = v.memset(digit[:, k:k + 1], float(1 << (ID_BITS * k)))
            step(ins)
            step(v.tensor_tensor(shifted[:], tile_expert[:].rearrange("a (g k) -> a g k", k=IDS),
                                 digit[:].unsqueeze(1).broadcast_to([1, WORDS, IDS]), ALU.mult))
            step(v.tensor_reduce(word_f[:], shifted[:], AX, ALU.add))
            v.tensor_copy(word[:], word_f[:]).then_inc(words_done, 1)
            def tile_lo(q, k):
                J = RING * q + k
                dve.wait_ge(a_t, J + 1)
                need(dve, pe_gu, J - 1)
                sub(gT_lo[:, k % 2, :], bank[:, k % 2, 0:D], gT_hi[:, k % 2, :]).then_inc(d_t, 1)

            def tile_lo_routed(q, k):
                tile_lo(q, k)
                need(dve, sc_y[k], 16 * (q - q_routed))
                v.tensor_copy(dest[:, k:k + 1], ring[:, k, D:D + 1].bitcast(U32)).then_inc(d_dest, 1)
                v.tensor_copy(gate[:, k:k + 1], ring[:, k, D + 1:D + 2]).then_inc(d_dest, 1)

            def hidden(q, k):
                J = RING * q + k
                dve.wait_ge(a_silu, J + 1)
                need(dve, pe_hT, J - 1)
                v.tensor_tensor(h[:, k % 2, :], sg[:, k % 2, :], bank[:, 2 + k % 2, I:2 * I], ALU.mult).then_inc(d_h, 1)

            def hidden_lo(q, k):
                J = RING * q + k
                dve.wait_ge(a_hT, J + 1)
                need(dve, pe_y, J - 1)
                sub(hT_lo[:, k % 2, :], bank[:, 4 + k % 2, 0:P], hT_hi[:, k % 2, :]).then_inc(d_hT, 1)

            def add_shared(q, k):
                J = RING * q + k
                dve.wait_ge(pe_y, J + 1)
                need(dve, d_y, J)
                r = res[:, bass.ds(RING // HALVES * q + k // HALVES, 1), :].rearrange("p a d -> p (a d)")
                v.scalar_tensor_tensor(out=r, in0=bank[:, 6 + k % 2, 0:D], scalar=SHARED_RATIO, in1=r,
                                       op0=ALU.mult, op1=ALU.add).then_inc(d_y, 1)

            def keep_results(q, k):
                J = RING * q + k
                dve.wait_ge(pe_y, J + 1)
                v.tensor_scalar(y_sb[:, k, :], bank[:, 6 + k % 2, 0:D], gate[:, k:k + 1], None, ALU.mult).then_inc(d_y, 1)

            pipelined(dve, q_shared, SHARED_STEPS // RING, [(1, tile_lo), (0, hidden), (-1, hidden_lo), (-2, add_shared)])
            pipelined(dve, q_routed, GROUPS, [(1, tile_lo_routed), (0, hidden), (-1, hidden_lo), (-2, keep_results)])

            for b in range(B):
                r = res[:, b * BT:(b + 1) * BT, :]
                dve.wait_ge(ld_both[b % 2], 16 * (b // 2 + 1))
                v.tensor_tensor(r, r, both[:, b % 2, :, 0, :], ALU.add).then_inc(f_part, 1)
                dve.wait_ge(f_part, b + 1)
                v.tensor_tensor(r, r, both[:, b % 2, :, 1, :], ALU.add).then_inc(f_done, 1)

        @block.tensor
        def _(pe):
            def transpose_rows(src, made):
                for c in range(KC):
                    for t in range(BT):
                        ins = pe.transpose(bank[:, 4 + c, t * P:(t + 1) * P], src[:, t, c * P:(c + 1) * P], ident[:])
                    ins.then_inc(made, 1)

            pe.wait_ge(ld_wqk, 32)
            pe.wait_ge(consts, 1)
            for n in range(2):
                for c in range(KC):
                    for r in range(KC):
                        ins = pe.transpose(bank[:, n, c * D + r * P:c * D + (r + 1) * P],
                                           wqk_raw[:, n, r, c * P:(c + 1) * P], ident[:])
                ins.then_inc(wT_done, 1)
            pe.wait_ge(ln1_done, BT)
            transpose_rows(xn, pe_xT)
            pe.wait_ge(ld_cen, 16)
            for c in range(KC):
                ins = pe.transpose(bank[:, 3, c * E:(c + 1) * E], cen_raw[:, c * P:(c + 1) * P], ident[0:E, 0:E])
            ins.then_inc(cenT, 1)
            pe.wait_ge(wT_copied, 2)
            for r in range(KC):
                for c in range(KC):
                    ins = pe.matmul(bank[:, 2, r * D:(r + 1) * D], wqkT[:, 0, c, r * P:(r + 1) * P], wqkT[:, 1, c, :],
                                    start=(c == 0), stop=(c == KC - 1))
            ins.then_inc(a_done, 1)
            pe.wait_ge(a_lo_done, 1)
            pe.wait_ge(wv_done, 2)
            pe.wait_ge(cen_done, 1)

            def wide(cen):
                return cen.unsqueeze(1).broadcast_to([P, D // E, E])

            def logits(b):
                pe.wait_ge(d_x2T, KC * (b + 1))
                for n in range(2):
                    for t in (2 * n, 2 * n + 1):
                        for c in range(KC):
                            at = slice(t * P, (t + 1) * P)
                            ins = split3(pe, bank[:, 4 + n, t % 2 * D:(t % 2 + 1) * D], x2T_hi[:, c, at], x2T_lo[:, c, at],
                                         wide(cen_hi[:, c, :]), wide(cen_lo[:, c, :]), c == 0, c == KC - 1)
                    ins.then_inc(pe_logit, 1)

            def batch(b, first, last):
                pe.wait_ge(d_xT, KC * (b + 1))
                need(pe, d_pT, BT * b)
                for n in range(2):
                    for t in (2 * n, 2 * n + 1):
                        for c in range(KC):
                            at = slice(t * P, (t + 1) * P)
                            ins = split3(pe, bank[:, n, t % 2 * D:(t % 2 + 1) * D], xT_hi[:, c, at], xT_lo[:, c, at],
                                         wv_hi[:, c, :], wv_lo[:, c, :], c == 0, c == KC - 1)
                    ins.then_inc(pe_v, 1)
                need(pe, d_o, BT * b)
                for m in range(KC):
                    for c in range(KC):
                        at = slice(m * P, (m + 1) * P)
                        ins = split3(pe, bank[:, 2 + m, :], a_hi[:, c, at], a_lo[:, c, at], xT_hi[:, c, :], xT_lo[:, c, :],
                                     c == 0, c == KC - 1)
                    ins.then_inc(pe_qT, 1)
                if not first:
                    pe.wait_ge(ln2_done, BT * b)
                    transpose_rows(x2, pe_x2T)

                def scores(n):
                    i = BT - 1 - n
                    need(pe, a_exp, BT * b + max(n - 1, 0))
                    s = bank[:, 6 + n % 2, :]
                    cols = max((i + 1) * P, 2 * P)
                    at = slice(i * P, (i + 1) * P)
                    for m in range(KC):
                        split3(pe, s[:, 0:cols], qT_hi[:, m, at], qT_lo[:, m, at], xT_hi[:, m, 0:cols],
                               xT_lo[:, m, 0:cols], m == 0, False)
                    pe.matmul(s[:, at], ident_b[:], mask_b[:], start=False, stop=True).then_inc(pe_s, 1)

                def probsT(n):
                    pe.wait_ge(a_exp, BT * b + n + 1)
                    if n > 1:
                        pe.wait_ge(d_pT, BT * b + n - 1)
                    for kb in range(BT - n):
                        at = slice(kb * P, (kb + 1) * P)
                        ins = pe.transpose(bank[:, n % 2, at], probs[:, n % 2, at], ident[:])
                    ins.then_inc(pe_pT, 1)

                def attend(n):
                    pe.wait_ge(d_pT, BT * b + n + 1)
                    if n > 1:
                        pe.wait_ge(d_o, BT * b + n - 1)
                    for kb in range(BT - n):
                        at = slice(kb * P, (kb + 1) * P)
                        ins = split3(pe, bank[:, 2 + n % 2, 0:D], pT_hi[:, n % 2, at], pT_lo[:, n % 2, at],
                                     v_hi[:, kb, :], v_lo[:, kb, :], kb == 0, kb == BT - 1 - n)
                    ins.then_inc(pe_o, 1)

                pe.wait_ge(d_qT, KC * (b + 1))
                scores(0)
                scores(1)
                if not first:
                    logits(b - 1)
                pe.wait_ge(d_v, 2 * (b + 1))
                probsT(0)
                scores(2)
                attend(0)
                probsT(1)
                scores(3)
                attend(1)
                probsT(2)
                if not last:
                    pe.wait_ge(ln1_done, BT * (b + 2))
                    if not first:
                        pe.wait_ge(d_logit, 2 * b)
                    transpose_rows(xn, pe_xT)
                attend(2)
                probsT(3)
                attend(3)

            over_batches(pe, batch)
            pe.wait_ge(ln2_done, BT * B)
            transpose_rows(x2, pe_x2T)
            logits(B - 1)

            pe.wait_ge(hot_done, 2)
            pe.matmul(bank[:, 7, 0:(TILES + 1) * E], before_b[:], hot_b[:].rearrange("p t e -> p (t e)"), start=True, stop=False)
            for t in range(TILES):
                n = TILES - t
                ins = pe.matmul(bank[:, 7, (t + 1) * E:(TILES + 1) * E].rearrange("p (t e) -> p t e", e=E), ones_b[:],
                                hot_b[:, t:t + 1, :].broadcast_to([P, n, E]), start=False, stop=(t == TILES - 1))
            ins.then_inc(ranks, 1)

            def transpose_tile(q, k):
                J = RING * q + k
                pe.wait_ge(ld_t[k], 16 * (q + 1))
                need(pe, d_t, J - 1)
                for c in range(KC):
                    ins = pe.transpose(bank[:, k % 2, c * P:(c + 1) * P], ring[:, k, c * P:(c + 1) * P], ident[:])
                ins.then_inc(pe_t, 1)

            def weights_of(e, at):
                if isinstance(e, int):
                    return w_hi[:, e, at], w_lo[:, e, at]
                return w_hi[:, bass.ds(e, 1), at], w_lo[:, bass.ds(e, 1), at]

            def gate_up(q, k, e):
                J = RING * q + k
                pe.wait_ge(d_t, J + 1)
                need(pe, d_h, J - 1)
                for c in range(KC):
                    at = slice(c * P, (c + 1) * P)
                    rhi, rlo = weights_of(e, slice(c * 2 * I, (c + 1) * 2 * I))
                    ins = split3(pe, bank[:, 2 + k % 2, 0:2 * I], gT_hi[:, k % 2, at], gT_lo[:, k % 2, at], rhi, rlo,
                                 c == 0, c == KC - 1)
                ins.then_inc(pe_gu, 1)

            def hidden_T(q, k):
                J = RING * q + k
                pe.wait_ge(d_h, J + 1)
                need(pe, d_hT, J - 1)
                pe.transpose(bank[:, 4 + k % 2, 0:P], h[:, k % 2, :], ident[:]).then_inc(pe_hT, 1)

            def down(q, k, e):
                J = RING * q + k
                pe.wait_ge(d_hT, J + 1)
                need(pe, d_y, J - 1)
                rhi, rlo = weights_of(e, slice(KC * 2 * I, WE))
                split3(pe, bank[:, 6 + k % 2, 0:D], hT_hi[:, k % 2, :], hT_lo[:, k % 2, :], rhi, rlo, True, True)\
                    .then_inc(pe_y, 1)

            pe.wait_ge(w_lo_done, E + HALVES)
            pe.wait_ge(slots_done, 1)
            pipelined(pe, q_shared, SHARED_STEPS // RING,
                      [(1, transpose_tile), (0, lambda q, k: gate_up(q, k, E + k % 2)), (-1, hidden_T),
                       (-2, lambda q, k: down(q, k, E + k % 2))])

            pe.wait_ge(words_done, 1)
            words = {}

            def load_words(q):
                for n in range(-1, RING // IDS):
                    at = RING // IDS * (q - q_routed) + n
                    if isinstance(at, int) and not 0 <= at < WORDS:
                        continue
                    words[n] = pe.snap(pe.value_load(word[0:1, bass.ds(at, 1)]))

            def expert(j):
                return pe.snap((words[j // IDS] >> (ID_BITS * (j % IDS))) & (E - 1), min_val=0, max_val=E - 1)

            def routed_gate_up(q, k):
                gate_up(q, k, expert(position[0]))

            def routed_down(q, k):
                down(q, k, expert(position[0]))

            pipelined(pe, q_routed, GROUPS,
                      [(1, transpose_tile), (0, routed_gate_up), (-1, hidden_T), (-2, routed_down)], load_words)


_INS = ['L0_attn_x', 'L0_attn_Wq', 'L0_attn_Wk', 'L0_attn_Wv', 'L0_ffn_centroids', 'L0_ffn_gate_bias', 'L0_ffn_wg_s',
        'L0_ffn_wu_s', 'L0_ffn_wd_s', 'L0_ffn_wg', 'L0_ffn_wu', 'L0_ffn_wd']
_OUTS = [((4, 512, 256), 'float32')]


def kernel(**inputs):
    import numpy as _np
    import concourse.bacc as _bacc
    from concourse import mybir as _mybir
    from concourse.bass_utils import run_bass_kernel_spmd as _run

    nc = _bacc.Bacc("TRN2", target_bir_lowering=False, num_devices=1)
    arrays, args = {}, []
    for name in _INS:
        a = _np.ascontiguousarray(inputs[name])
        arrays[f"in_{name}_dram"] = a
        args.append(nc.dram_tensor(f"in_{name}_dram", a.shape, _mybir.dt.from_np(a.dtype), kind="ExternalInput").ap())
    for i, (shape, dtype) in enumerate(_OUTS):
        dt = _mybir.dt.from_np(_np.dtype(dtype))
        args.append(nc.dram_tensor(f"out_{i}_dram", shape, dt, kind="ExternalOutput").ap())
    block_causal_attention_and_moe(nc, *args)
    r = _run(nc, [arrays], core_ids=[0])
    got = tuple(r.results[0][f"out_{i}_dram"] for i in range(len(_OUTS)))
    return got[0]
```

```python
from contextlib import ExitStack

import concourse.bass as bass
from concourse import mybir

P = 128
ALU = mybir.AluOpType
ACT = mybir.ActivationFunctionType
AX = mybir.AxisListType.X
F32 = mybir.dt.float32
F32R = mybir.dt.float32r
BF16 = mybir.dt.bfloat16
U32 = mybir.dt.uint32
I32 = mybir.dt.int32

LEAST_LOGIT = -87.0
LN_EPS = 1e-5
GATE_EPS = 1e-9
SHARED_RATIO = 0.1
MASKED = -1e30

RING = 8
ID_BITS = 4
IDS = 8


def block_causal_attention_and_moe(
    nc: bass.Bass, x, Wq, Wk, Wv, centroids, gate_bias, wg_s, wu_s, wd_s, wg, wu, wd, out
):
    B, S, D = x.shape
    E, _, I = wg.shape
    TILES = B * S // P
    BT = S // P
    KC = D // P
    HALVES = wg_s.shape[1] // I
    assert D == 256 and I == P and BT == 4 and E == 16 and HALVES == 2
    SCALE = float(D) ** -0.5
    EXPERT_TILES = 2 * TILES + E
    GROUPS = EXPERT_TILES // RING
    WORDS = EXPERT_TILES // IDS
    LIST_TILES = TILES + 1
    IDLE_TILES = EXPERT_TILES - 2 * TILES
    LIST_ROWS = LIST_TILES * P
    ROW = D + 2
    WE = KC * 2 * I + D
    CT = 2
    CHUNKS = TILES // CT
    RESULTS = 2 * TILES * P

    expert_rows = nc.dram_tensor("expert_rows", (E * LIST_ROWS + IDLE_TILES * P, ROW), F32, kind="Internal").ap()
    expert_out = nc.dram_tensor("expert_out", (RESULTS, D), F32, kind="Internal").ap()

    ctx = ExitStack()
    with ctx:
        def sb(name, shape, dt=F32):
            return ctx.enter_context(nc.sbuf_tensor(name, shape, dt))

        def sem(name):
            return ctx.enter_context(nc.semaphore(name))

        res = sb("res", [P, TILES, D])
        rows = sb("rows", [P, 2, BT, ROW])
        wv_raw = rows[:, 0].rearrange("p t r -> p (t r)")[:, 0:KC * D].rearrange("p (c n) -> p c n", c=KC)
        cen_raw = rows[:, 1].rearrange("p t r -> p (t r)")[0:E, 0:D]
        padding = rows[:, 0, BT - 1, :]
        w_hi = sb("w_hi", [P, E + HALVES, WE], F32R)
        w_lo = sb("w_lo", [P, E + HALVES, WE], F32R)
        w_raw = sb("w_raw", [P, 2, WE])
        ident = sb("ident", [P, P])
        ident_b = sb("ident_b", [P, P], BF16)
        mask_b = sb("mask_b", [P, P], BF16)
        before_b = sb("before_b", [P, P], BF16)
        ones_b = sb("ones_b", [P, P], BF16)
        a_hi = sb("a_hi", [P, KC, D], F32R)
        a_lo = sb("a_lo", [P, KC, D], F32R)
        wv_hi = sb("wv_hi", [P, KC, D], F32R)
        wv_lo = sb("wv_lo", [P, KC, D], F32R)
        cen_hi = sb("cen_hi", [P, KC, E], F32R)
        cen_lo = sb("cen_lo", [P, KC, E], F32R)
        mv1 = sb("mv1", [P, TILES, 2])
        veps1 = sb("veps1", [P, TILES])
        rstd1 = sb("rstd1", [P, TILES])
        stats2 = sb("stats2", [P, BT, 6])
        mv2 = sb("mv2", [P, BT, 2])
        veps2 = sb("veps2", [P, BT])
        rstd2 = sb("rstd2", [P, BT])
        minus_half = sb("minus_half", [P, TILES])
        smax = sb("smax", [P, BT])
        nbias = sb("nbias", [P, BT])
        rsum = sb("rsum", [P, BT])
        rinv = sb("rinv", [P, BT])
        en = sb("en", [P, BT, E])
        logit = sb("logit", [P, BT, E])
        bias_all = sb("bias_all", [P, E])
        result_row = sb("result_row", [P, 2, BT], U32)
        iota_u = sb("iota_u", [P, EXPERT_TILES], I32)
        list_u = sb("list_u", [P, E], I32)
        ones_e = sb("ones_e", [P, E])
        weight = sb("weight", [P, 2, BT])
        list_at = sb("list_at", [P, E])
        aff = sb("aff", [P, BT, E])
        biased = sb("biased", [P, BT, E])
        top8 = sb("top8", [P, BT, 8])
        top8_at = sb("top8_at", [P, BT, 8], U32)
        top_at = sb("top_at", [P, 2, BT])
        iota_f = sb("iota_f", [P, EXPERT_TILES])
        hot = sb("hot", [P, 2, BT, E])
        picked = sb("picked", [P, 2, BT, E])
        stats1 = picked[:].rearrange("p c t e -> p (c t e)")[:, 0:TILES * 6].rearrange("p (t s) -> p t s", t=TILES)
        hot_b = sb("hot_b", [P, BT + 1, E], BF16)
        in_batch = sb("in_batch", [P, E])
        hot_sum = sb("hot_sum", [P, E], BF16)
        taff = sb("taff", [P, 2, BT])
        tsum = sb("tsum", [P, BT])
        pos = biased
        slot_f = sb("slot_f", [P, 2, BT])
        slot_u = sb("slot_u", [P, 2, BT], U32)

        with ExitStack() as attention:
            def asb(name, shape, dt=F32):
                return attention.enter_context(nc.sbuf_tensor(name, shape, dt))

            xn = asb("xn", [P, BT, D])
            x2 = asb("x2", [P, BT, D])
            probs = asb("probs", [P, 2, S])
            wqkT = x2[:].rearrange("p (w c) n -> p w c n", w=2)
            xT_hi = asb("xT_hi", [P, KC, S], F32R)
            xT_lo = asb("xT_lo", [P, KC, S], F32R)
            qT_hi = asb("qT_hi", [P, KC, S], F32R)
            qT_lo = asb("qT_lo", [P, KC, S], F32R)
            v_hi = asb("v_hi", [P, BT, D], F32R)
            v_lo = asb("v_lo", [P, BT, D], F32R)
            pT_hi = asb("pT_hi", [P, 2, S], F32R)
            pT_lo = asb("pT_lo", [P, 2, S], F32R)
            x2T_hi, x2T_lo = pT_hi, pT_lo
            logit_T = xn[0:E, 0:2, :].rearrange("p t d -> p (t d)")
            hs_hi = asb("hs_hi", [P, HALVES, S], F32R)
            hs_lo = asb("hs_lo", [P, HALVES, S], F32R)
            hs = asb("hs", [P, HALVES, S])
            wqk_raw = probs[:].rearrange("p w (c n) -> p w c n", c=KC)

        template = sb("template", [P, ROW])
        cnt = sb("cnt", [P, E])
        cnt_i = sb("cnt_i", [P, E], I32)
        tiles_f = sb("tiles_f", [P, E])
        ends = sb("ends", [P, E])
        gap = sb("gap", [P, E])
        pad_at = sb("pad_at", [P, E], U32)
        past = sb("past", [1, EXPERT_TILES, E])
        skipped = sb("skipped", [1, EXPERT_TILES, E])
        tile_f = sb("tile_f", [1, EXPERT_TILES])
        tile_at = sb("tile_at", [1, EXPERT_TILES], U32)
        tile_expert = sb("tile_expert", [1, EXPERT_TILES])
        digit = sb("digit", [1, IDS])
        shifted = sb("shifted", [1, WORDS, IDS])
        half_f = sb("half_f", [1, 2, WORDS])
        half_u = sb("half_u", [1, 2, WORDS], U32)
        word = sb("word", [1, WORDS], U32)
        ring = sb("ring", [P, RING, ROW])
        dest = sb("dest", [P, RING], U32)
        gate = sb("gate", [P, RING])
        gT_hi = sb("gT_hi", [P, 4, D], F32R)
        gT_lo = sb("gT_lo", [P, 4, D], F32R)
        sg = sb("sg", [P, 2, I])
        h = sb("h", [P, 2, I])
        hT_hi = sb("hT_hi", [P, 2, P], F32R)
        hT_lo = sb("hT_lo", [P, 2, P], F32R)
        y_sb = sb("y_sb", [P, RING, D])
        both = sb("both", [P, 4, CT, 2, D])

        bank = ctx.enter_context(nc.psum_tensor("bank", [P, 8, 512], F32))

        ld_wqk = sem("ld_wqk"); ld_wv = sem("ld_wv"); ld_cen = sem("ld_cen"); ld_bias = sem("ld_bias")
        ld_x = [sem(f"ld_x{b}") for b in range(B)]
        ld_w = [sem(f"ld_w{k}") for k in range(2)]
        filled = sem("filled")
        c_step = sem("c_step")
        consts = sem("consts")
        w_hi_done = sem("w_hi_done"); w_lo_done = sem("w_lo_done")
        wT_done = sem("wT_done"); wT_copied = sem("wT_copied"); a_done = sem("a_done")
        a_hi_done = sem("a_hi_done"); a_lo_done = sem("a_lo_done"); wv_done = sem("wv_done")
        cenT = sem("cenT"); cen_hi_done = sem("cen_hi_done"); cen_done = sem("cen_done")
        ln1_stats = sem("ln1_stats"); ln1_mv = sem("ln1_mv"); ln1_ve = sem("ln1_ve"); ln1_rstd = sem("ln1_rstd")
        ln1_done = sem("ln1_done")
        ln2_stats = sem("ln2_stats"); ln2_mv = sem("ln2_mv"); ln2_ve = sem("ln2_ve"); ln2_rstd = sem("ln2_rstd")
        ln2_done = sem("ln2_done")
        rows_copied = sem("rows_copied"); rows_named = sem("rows_named")
        rows_free = sem("rows_free")
        pe_xT = sem("pe_xT"); a_xT = sem("a_xT"); d_xT = sem("d_xT")
        pe_qT = sem("pe_qT"); a_qT = sem("a_qT"); d_qT = sem("d_qT")
        pe_v = sem("pe_v"); a_v = sem("a_v"); d_v = sem("d_v")
        pe_s = sem("pe_s"); d_max = sem("d_max"); d_nbias = sem("d_nbias"); a_exp = sem("a_exp")
        pe_pT = sem("pe_pT"); a_pT = sem("a_pT"); d_pT = sem("d_pT")
        pe_o = sem("pe_o"); d_rinv = sem("d_rinv"); d_o = sem("d_o")
        pe_x2T = sem("pe_x2T"); a_x2T = sem("a_x2T"); d_x2T = sem("d_x2T")
        pe_logit_T = sem("pe_logit_T"); a_logit_T = sem("a_logit_T"); pe_logit = sem("pe_logit"); d_logit = sem("d_logit"); a_en = sem("a_en")
        apart = sem("apart")
        r_step = sem("r_step")
        ROUTE_STEPS = 14
        sum_step = sem("sum_step")
        sum_done = sem("sum_done")
        hot_done = sem("hot_done"); ranks = sem("ranks"); ranks_read = sem("ranks_read")
        slots_done = sem("slots_done"); weights_done = sem("weights_done")
        pads_done = sem("pads_done"); template_made = sem("template_made"); padded = sem("padded"); tiles_done = sem("tiles_done"); words_done = sem("words_done")
        sent = sem("sent")
        pe_g = sem("pe_g"); pe_u = sem("pe_u"); a_gs = sem("a_gs"); d_hs = sem("d_hs")
        a_hs = sem("a_hs"); hs_split = sem("hs_split"); pe_down = sem("pe_down"); d_shared = sem("d_shared")
        ld_t = [sem(f"ld_t{k}") for k in range(RING)]
        pe_t = sem("pe_t"); a_t = sem("a_t"); d_t = sem("d_t"); d_dest = sem("d_dest")
        pe_gu = sem("pe_gu"); a_silu = sem("a_silu"); d_h = sem("d_h")
        pe_hT = sem("pe_hT"); a_hT = sem("a_hT"); d_hT = sem("d_hT")
        pe_y = sem("pe_y"); a_y = sem("a_y")
        sc_y = [sem(f"sc_y{k}") for k in range(RING)]
        ld_both = [sem(f"ld_both{k}") for k in range(4)]
        f_part = sem("f_part"); f_done = sem("f_done")
        stored = sem("stored")

        x_v = x.rearrange("b (t p) d -> b p t d", p=P)
        both_v = expert_out.rearrange("(n t p c) d -> n p t c d", n=CHUNKS, p=P, c=2)
        out_chunks = out.rearrange("b (n t p) d -> (b n) p t d", t=CT, p=P)

        def need(eng, s, v):
            if not isinstance(v, int) or v > 0:
                eng.wait_ge(s, v)

        def wait_apart(eng, s, v):
            eng.wait_ge(s, v)
            if not isinstance(v, int):
                eng.sem_inc(apart, 1)

        def over_batches(eng, body, after=None):
            body(0, first=True, last=False)
            with eng.Fori(1, B - 1) as b:
                body(b, first=False, last=False)
            body(B - 1, first=False, last=True)

        position = [0]

        def pipelined(eng, stages, begin=None):
            def group(q, first, last, extra=0):
                if begin:
                    begin(q)
                for k in range(RING + extra):
                    for lag, f in stages:
                        kk = k + lag
                        if first and kk < 0:
                            continue
                        if last and kk >= RING:
                            continue
                        if last and k >= RING and kk < 0:
                            continue
                        position[0] = kk
                        f(q + kk // RING, kk % RING)

            for lag, f in stages:
                for k in range(max(lag, 0)):
                    f(k // RING, k % RING)
            group(0, True, False)
            with eng.Fori(1, GROUPS - 1) as q:
                group(q, False, False)
            group(GROUPS - 1, False, True, extra=2)

        def split3(pe, acc, hi, lo, rhi, rlo, first, last):
            pe.matmul(acc, lo, rhi, start=first, stop=False)
            pe.matmul(acc, hi, rlo, start=False, stop=False)
            return pe.matmul(acc, hi, rhi, start=False, stop=last)

        SP_LISTS = 9

        def pad_lists(eng, first, end):
            eng.wait_ge(template_made, 1)
            eng.wait_ge(pads_done, 1)
            for e in range(first, end):
                row = eng.value_load(pad_at[0:1, e:e + 1], min_val=0, max_val=E * LIST_ROWS - P)
                eng.dma_start(expert_rows[bass.ds(row, P), :], template[:]).then_inc(padded, 16)

        STAT_TILES = [range(0, BT), range(BT, TILES - BT), range(TILES - BT, TILES)]

        block = ctx.enter_context(nc.Block())

        @block.sync
        def _(sp):
            sp.dma_start(res[:, 0:BT, :], x_v[0]).then_inc(ld_x[0], 16)
            for n, w in enumerate((Wq, Wk)):
                sp.dma_start(wqk_raw[:, n], w.rearrange("(c p) n -> p c n", p=P)).then_inc(ld_wqk, 16)
            sp.dma_start(wv_raw, Wv.rearrange("(c p) n -> p c n", p=P)).then_inc(ld_wv, 16)
            sp.dma_start(cen_raw, centroids).then_inc(ld_cen, 16)
            for b in range(1, B):
                sp.dma_start(res[:, b * BT:(b + 1) * BT, :], x_v[b]).then_inc(ld_x[b], 16)

            def gate_up(k, half):
                return w_raw[:, k, 0:KC * 2 * I].rearrange("p (c n) -> p c n", c=KC)[:, :, half * I:(half + 1) * I]

            for k in range(HALVES):
                for half, w in enumerate((wg_s, wu_s)):
                    sp.dma_start(gate_up(k, half), w[:, k * I:(k + 1) * I].rearrange("(c p) i -> p c i", p=P)).then_inc(ld_w[k], 16)
                sp.dma_start(w_raw[:, k, KC * 2 * I:WE], wd_s[k * I:(k + 1) * I, :]).then_inc(ld_w[k], 16)
            sp.dma_start(bias_all[:], gate_bias.rearrange("(a e) -> a e", a=1).broadcast_to([P, E])).then_inc(ld_bias, 16)

            sp.wait_ge(consts, 1)
            sp.dma_start(expert_rows[E * LIST_ROWS:, :].rearrange("(j p) r -> p j r", p=P),
                         padding.unsqueeze(1).broadcast_to([P, IDLE_TILES, ROW])).then_inc(filled, 16)

            with sp.Fori(0, E // 2) as m:
                for k in range(2):
                    e = 2 * m + k
                    sp.wait_ge(w_lo_done, e + HALVES - 1)
                    for half, w in enumerate((wg, wu)):
                        sp.dma_start(gate_up(k, half), w[bass.ds(e, 1)].rearrange("a (c p) i -> p (a c) i", p=P)).then_inc(ld_w[k], 16)
                    sp.dma_start(w_raw[:, k, KC * 2 * I:WE], wd[bass.ds(e, 1)].rearrange("a p d -> p (a d)")).then_inc(ld_w[k], 16)

            pad_lists(sp, 0, SP_LISTS)

            def first_row(q, k):
                return sp.value_load(tile_at[0:1, bass.ds(RING * q + k, 1)], min_val=0, max_val=E * LIST_ROWS + IDLE_TILES * P - P)

            def load_tile(k, row):
                sp.dma_start(ring[:, k, :], expert_rows[bass.ds(row, P), :]).then_inc(ld_t[k], 16)

            sp.wait_ge(tiles_done, 1)
            AHEAD = 3
            first_rows = [first_row(0, k) for k in range(AHEAD)]
            sp.wait_ge(filled, 16)
            sp.wait_ge(padded, 16 * E)
            sp.wait_ge(sent, 16 * 2 * TILES)
            for k in range(RING):
                load_tile(k, first_rows[k] if k < AHEAD else first_row(0, k))
            with sp.Fori(1, GROUPS) as q:
                for k in range(RING):
                    wait_apart(sp, d_dest, 2 * (RING * (q - 1) + k + 1))
                    wait_apart(sp, pe_t, RING * (q - 1) + k + 1)
                    load_tile(k, first_row(q, k))

            for k in range(RING):
                sp.wait_ge(sc_y[k], 16 * GROUPS)
            for n in range(CHUNKS):
                if n >= 4:
                    sp.wait_ge(f_done, n - 3)
                sp.dma_start(both[:, n % 4], both_v[n]).then_inc(ld_both[n % 4], 16)
            sp.wait_ge(stored, 16 * CHUNKS)

        @block.gpsimd
        def _(pool):
            g = nc.gpsimd
            done = [0]

            def step(ins):
                done[0] += 1
                ins.then_inc(c_step, 1)
                pool.wait_ge(c_step, done[0])

            def make_padding(rows_):
                step(g.memset(rows_, 0.0))
                step(g.iota(rows_[:, D:D + 1].bitcast(U32), pattern=[[0, 1]], base=RESULTS, channel_multiplier=1))

            step(g.memset(ident[:], 0.0))
            step(g.affine_select(out=ident[:], in_=ident[:], compare_op=ALU.not_equal, fill=1.0, base=0,
                                 pattern=[[-1, P]], channel_multiplier=1))
            step(g.memset(minus_half[:], -0.5))
            step(g.memset(mask_b[:], 0.0))
            step(g.affine_select(out=mask_b[:], in_=mask_b[:], compare_op=ALU.is_ge, fill=MASKED, base=0,
                                 pattern=[[-1, P]], channel_multiplier=1))
            step(g.memset(before_b[:], 1.0))
            step(g.affine_select(out=before_b[:], in_=before_b[:], compare_op=ALU.is_gt, fill=0.0, base=0,
                                 pattern=[[1, P]], channel_multiplier=-1))
            step(g.memset(ones_b[:], 1.0))
            make_padding(padding)
            step(g.iota(result_row[:], pattern=[[1, 2], [2 * P, BT]], base=0, channel_multiplier=2))
            step(g.iota(iota_u[:], pattern=[[1, EXPERT_TILES]], base=0, channel_multiplier=0))
            step(g.iota(list_u[:], pattern=[[LIST_ROWS, E]], base=0, channel_multiplier=0))
            step(g.tensor_copy(list_at[:], list_u[:]))
            step(g.tensor_copy(iota_f[:], iota_u[:]))
            step(g.memset(hot_sum[:], 0.0))
            step(g.memset(hot_b[:, BT, :], 0.0))
            step(g.tensor_copy(ident_b[:], ident[:]))
            g.memset(ones_e[:], 1.0).then_inc(consts, 1)

            def rsqrt(nth, tiles, mean_var, plus_eps, rs, mv_ready, added, ready):
                n = tiles.stop - tiles.start
                wait_apart(pool, mv_ready, nth + 1)
                g.tensor_scalar(plus_eps[:, tiles], mean_var[:, tiles, 1], LN_EPS, None, ALU.add).then_inc(added, 1)
                wait_apart(pool, added, nth + 1)
                g.tensor_tensor(rs[:, tiles], plus_eps[:, tiles], minus_half[:, 0:n], ALU.pow).then_inc(ready, 1)

            def weights_lo(s, e, k):
                wait_apart(pool, w_hi_done, s + 1)
                g.tensor_tensor(w_lo[:, bass.ds(e, 1), :], w_raw[:, k:k + 1, :], w_hi[:, bass.ds(e, 1), :].bitcast(F32),
                                ALU.subtract).then_inc(w_lo_done, 1)

            def shared_lo(b):
                for half in range(HALVES):
                    wait_apart(pool, a_hs, HALVES * b + half + 1)
                    g.tensor_tensor(hs_lo[:, half, :], hs[:, half, :], hs_hi[:, half, :].bitcast(F32),
                                    ALU.subtract).then_inc(hs_split, 1)

            def name_rows(b):
                pool.wait_ge(filled, 16)
                wait_apart(pool, weights_done, b + 1)
                g.tensor_copy(rows[:, :, :, D].bitcast(U32), result_row[:]).then_inc(rows_named, 1)
                g.tensor_copy(rows[:, :, :, D + 1], weight[:]).then_inc(rows_named, 1)
                wait_apart(pool, rows_named, 3 * b + 2)
                g.tensor_scalar(result_row[:], result_row[:], float(2 * BT * P), None, ALU.add).then_inc(rows_named, 1)

            def send_rows(b):
                wait_apart(pool, rows_named, 3 * b + 3)
                wait_apart(pool, rows_copied, 2 * (b + 1))
                wait_apart(pool, slots_done, b + 1)
                for c in range(2):
                    for t in range(BT):
                        g.indirect_dma_start(expert_rows, bass.IndirectOffsetOnAxis(slot_u[:, c, t:t + 1], 0),
                                             rows[:, c, t, :], None).then_inc(sent, 16)

            def free_rows(b):
                pool.wait_ge(sent, 16 * 2 * BT * (b + 1))
                pool.sem_inc(rows_free, 1)

            pool.sem_inc(rows_free, 1)
            for nth, tiles in enumerate(STAT_TILES):
                rsqrt(nth, slice(tiles.start, tiles.stop), mv1, veps1, rstd1, ln1_mv, ln1_ve, ln1_rstd)
            for n in range(HALVES):
                weights_lo(n, E + n, n)

            def batch(b, first, last):
                weights_lo(HALVES + BT * b, BT * b, 0)
                if not first:
                    shared_lo(b - 1)
                for n in range(1, BT - 1):
                    weights_lo(HALVES + BT * b + n, BT * b + n, n % 2)
                if not first:
                    name_rows(b - 1)
                rsqrt(b, slice(0, BT), mv2, veps2, rstd2, ln2_mv, ln2_ve, ln2_rstd)
                if last:
                    send_rows(b - 1)
                weights_lo(HALVES + BT * b + BT - 1, BT * b + BT - 1, (BT - 1) % 2)
                if not first and not last:
                    send_rows(b - 1)
                if not first:
                    free_rows(b - 1)

            over_batches(pool, batch)
            pool.wait_ge(pe_logit, B)
            step(g.memset(template[:], 0.0))
            g.iota(template[:, D:D + 1].bitcast(U32), pattern=[[0, 1]], base=RESULTS, channel_multiplier=1).then_inc(template_made, 1)
            name_rows(B - 1)
            send_rows(B - 1)

            def scatter_results(q, k):
                wait_apart(pool, a_y, RING * q + k + 1)
                g.indirect_dma_start(expert_out, bass.IndirectOffsetOnAxis(dest[:, k:k + 1], 0),
                                     y_sb[:, k, :], None, bounds_check=RESULTS - 1, oob_is_err=False).then_inc(sc_y[k], 16)

            with pool.Fori(0, GROUPS) as q:
                for k in range(RING):
                    scatter_results(q, k)

        @block.scalar
        def _(act):
            a = nc.scalar

            def weights_hi(s, e, k, nth):
                act.wait_ge(ld_w[k], 48 * (nth + 1))
                a.activation(w_hi[:, bass.ds(e, 1), :], w_raw[:, k:k + 1, :], ACT.Copy).then_inc(w_hi_done, 1)

            def transposed(b, made, mine, hi, at, freed, freed_at, chunks=range(KC)):
                need(act, freed, freed_at)
                for c in chunks:
                    act.wait_ge(made, KC * b + c + 1)
                    a.activation(hi[:, c, :], bank[:, at + c, :], ACT.Copy).then_inc(mine, 1)

            def copy_logits(b, at=4):
                act.wait_ge(pe_logit_T, b + 1)
                a.activation(logit_T, bank[0:E, at, :], ACT.Copy).then_inc(a_logit_T, 1)

            def gates(b):
                act.wait_ge(d_logit, b + 1)
                a.activation(en[:], logit[:], ACT.Exp, scale=-1.0).then_inc(a_en, 1)

            def copy_rows(b):
                act.wait_ge(filled, 16)
                wait_apart(act, rows_free, b + 1)
                wait_apart(act, ln2_done, BT * (b + 1))
                for c in range(2):
                    a.activation(rows[:, c, :, 0:D], x2[:], ACT.Copy).then_inc(rows_copied, 1)

            def shared_silu(b):
                for half in range(HALVES):
                    act.wait_ge(pe_g, HALVES * b + half + 1)
                    a.activation(hs[:, half, :], bank[:, half, :], ACT.Silu).then_inc(a_gs, 1)

            def shared_hi(b):
                for half in range(HALVES):
                    act.wait_ge(d_hs, HALVES * b + half + 1)
                    a.activation(hs_hi[:, half, :], hs[:, half, :], ACT.Copy).then_inc(a_hs, 1)

            def batch(b, first, last):
                need(act, pe_o, BT * b)
                for n in range(2):
                    act.wait_ge(pe_v, 2 * b + n + 1)
                    a.activation(v_hi[:, 2 * n:2 * n + 2, :].rearrange("p t d -> p (t d)"), bank[:, n, :],
                                 ACT.Copy).then_inc(a_v, 1)
                for m in range(KC):
                    act.wait_ge(pe_qT, KC * b + m + 1)
                    a.activation(qT_hi[:, m, :], bank[:, 2 + m, :], ACT.Copy).then_inc(a_qT, 1)
                if not first:
                    transposed(b - 1, pe_x2T, a_x2T, x2T_hi, 4, pe_o, BT * b)

                def exps(n):
                    i, cols = BT - 1 - n, (BT - n) * P
                    act.wait_ge(d_nbias, BT * b + n + 1)
                    need(act, pe_pT, BT * b + max(n - 1, 0))
                    a.activation(probs[:, n % 2, 0:cols], bank[:, 6 + n % 2, 0:cols], ACT.Exp, bias=nbias[:, i:i + 1],
                                 scale=SCALE, accum_out=rsum[:, i:i + 1]).then_inc(a_exp, 1)

                def probsT(n):
                    cols = (BT - n) * P
                    act.wait_ge(pe_pT, BT * b + n + 1)
                    need(act, pe_o, BT * b + max(n - 1, 0))
                    a.activation(pT_hi[:, n % 2, 0:cols], bank[:, n % 2, 0:cols], ACT.Copy).then_inc(a_pT, 1)

                exps(0)
                if not first:
                    copy_logits(b - 1)
                exps(1)
                if not first:
                    gates(b - 1)
                weights_hi(HALVES + BT * b, BT * b, 0, 2 * b + 1)
                if not first:
                    shared_silu(b - 1)
                probsT(0)
                exps(2)
                weights_hi(HALVES + BT * b + 1, BT * b + 1, 1, 2 * b + 1)
                if not first:
                    shared_hi(b - 1)
                probsT(1)
                exps(3)
                weights_hi(HALVES + BT * b + 2, BT * b + 2, 0, 2 * b + 2)
                probsT(2)
                if not last:
                    transposed(b + 1, pe_xT, a_xT, xT_hi, 6, pe_s, BT * (b + 1), [0])
                probsT(3)
                if not last:
                    transposed(b + 1, pe_xT, a_xT, xT_hi, 6, pe_s, BT * (b + 1), [1])
                if not first:
                    copy_rows(b - 1)
                weights_hi(HALVES + BT * b + 3, BT * b + 3, 1, 2 * b + 2)

            act.wait_ge(ld_wv, 16)
            a.activation(wv_hi[:], wv_raw, ACT.Copy).then_inc(wv_done, 1)
            for n in range(2):
                act.wait_ge(wT_done, n + 1)
                a.activation(wqkT[:, n].rearrange("p c n -> p (c n)"), bank[:, n, :], ACT.Copy).then_inc(wT_copied, 1)
            transposed(0, pe_xT, a_xT, xT_hi, 6, None, 0)
            act.wait_ge(a_done, 1)
            a.activation(a_hi[:].rearrange("p c n -> p (c n)"), bank[:, 2, :], ACT.Copy).then_inc(a_hi_done, 1)
            act.wait_ge(cenT, 1)
            a.activation(cen_hi[:], bank[:, 3, 0:KC * E].rearrange("p (c e) -> p c e", c=KC),
                         ACT.Copy).then_inc(cen_hi_done, 1)
            for n in range(HALVES):
                weights_hi(n, E + n, n, 0)
            over_batches(act, batch)
            transposed(B - 1, pe_x2T, a_x2T, x2T_hi, 6, pe_o, BT * B)
            copy_logits(B - 1, 2)
            gates(B - 1)
            shared_silu(B - 1)
            copy_rows(B - 1)
            shared_hi(B - 1)
            pad_lists(act, SP_LISTS, E)

            def tile_hi(q, k):
                J = RING * q + k
                act.wait_ge(pe_t, J + 1)
                a.activation(gT_hi[:, k % 4, :], bank[:, k % 2, 0:D], ACT.Copy).then_inc(a_t, 1)

            def silu(q, k):
                J = RING * q + k
                act.wait_ge(pe_gu, J + 1)
                a.activation(sg[:, k % 2, :], bank[:, 2 + k % 2, 0:I], ACT.Silu).then_inc(a_silu, 1)

            def hidden_hi(q, k):
                J = RING * q + k
                act.wait_ge(pe_hT, J + 1)
                a.activation(hT_hi[:, k % 2, :], bank[:, 4 + k % 2, 0:P], ACT.Copy).then_inc(a_hT, 1)

            def keep_results(q, k):
                J = RING * q + k
                act.wait_ge(pe_y, J + 1)
                if not isinstance(q, int) or q > 0:
                    act.wait_ge(sc_y[k], 16 * q)
                a.activation(y_sb[:, k, :], bank[:, 6 + k % 2, 0:D], ACT.Copy, scale=gate[:, k:k + 1]).then_inc(a_y, 1)

            pipelined(act, [(2, tile_hi), (0, silu), (-1, hidden_hi), (-2, keep_results)])

            for n in range(CHUNKS):
                act.wait_ge(f_done, n + 1)
                act.dma_start(out_chunks[n], res[:, n * CT:(n + 1) * CT, :]).then_inc(stored, 16)

        @block.vector
        def _(dve):
            v = nc.vector

            def res_tile(b, t):
                return res[:, bass.ds(BT * b + t, 1), :].rearrange("p a d -> p (a d)") if not isinstance(b, int) \
                    else res[:, BT * b + t, :]

            def stats_of_inputs(tiles):
                for t in tiles:
                    v.bn_stats(stats1[:, t, :], res[:, t, :]).then_inc(ln1_stats, 1)
                dve.wait_ge(ln1_stats, tiles[-1] + 1)
                for t in tiles:
                    ins = v.bn_aggr(mv1[:, t, :], stats1[:, t, :])
                ins.then_inc(ln1_mv, 1)

            def normalized_input(b):
                dve.wait_ge(ln1_rstd, 1 if isinstance(b, int) and b == 0 else len(STAT_TILES))
                need(dve, pe_xT, KC * b)
                for t in range(BT):
                    at = BT * b + t
                    one = slice(at, at + 1) if isinstance(b, int) else bass.ds(at, 1)
                    v.tensor_scalar(xn[:, t, :], res_tile(b, t), mv1[:, one, 0], rstd1[:, one],
                                    ALU.subtract, ALU.mult).then_inc(ln1_done, 1)

            def batch_stats(b):
                wait_apart(dve, ln2_stats, BT * (b + 1))
                for t in range(BT):
                    ins = v.bn_aggr(mv2[:, t, :], stats2[:, t, :])
                ins.then_inc(ln2_mv, 1)

            def normalized(b):
                dve.wait_ge(ln2_rstd, b + 1)
                for t in range(BT):
                    v.tensor_scalar(x2[:, t, :], res_tile(b, t), mv2[:, t, 0:1], rstd2[:, t:t + 1],
                                    ALU.subtract, ALU.mult).then_inc(ln2_done, 1)

            def sub(dst, src, hi):
                return v.tensor_tensor(dst, src, hi.bitcast(F32), ALU.subtract)

            def transposed(b, his, mine, lo, hi, at, freed, freed_at, chunks=range(KC)):
                need(dve, freed, freed_at)
                for c in chunks:
                    dve.wait_ge(his, KC * b + c + 1)
                    sub(lo[:, c, :], bank[:, at + c, :], hi[:, c, :]).then_inc(mine, 1)

            dve.wait_ge(ld_x[0], 16)
            stats_of_inputs(STAT_TILES[0])
            normalized_input(0)
            dve.wait_ge(wv_done, 1)
            sub(wv_lo[:], wv_raw, wv_hi[:]).then_inc(wv_done, 1)
            transposed(0, a_xT, d_xT, xT_lo, xT_hi, 6, None, 0)
            for b in range(1, B - 1):
                dve.wait_ge(ld_x[b], 16)
            stats_of_inputs(STAT_TILES[1])
            dve.wait_ge(a_hi_done, 1)
            sub(a_lo[:].rearrange("p c n -> p (c n)"), bank[:, 2, :], a_hi[:].rearrange("p c n -> p (c n)")).then_inc(a_lo_done, 1)
            dve.wait_ge(cen_hi_done, 1)
            sub(cen_lo[:], bank[:, 3, 0:KC * E].rearrange("p (c e) -> p c e", c=KC), cen_hi[:]).then_inc(cen_done, 1)
            dve.wait_ge(ld_x[B - 1], 16)
            stats_of_inputs(STAT_TILES[2])

            n_step = [0]

            def step(ins):
                n_step[0] += 1
                ins.then_inc(r_step, 1)
                wait_apart(dve, r_step, step_base[0] + n_step[0])

            step_base = [0]

            def over_e(ap):
                return ap.unsqueeze(3).broadcast_to([P, 2, BT, E])

            def both_experts(ap):
                return ap.unsqueeze(1).broadcast_to([P, 2, BT, E])

            def choose(b):
                step_base[0], n_step[0] = ROUTE_STEPS * b, 0
                if isinstance(b, int) and b == 0:
                    dve.wait_ge(ld_bias, 16)
                wait_apart(dve, a_en, b + 1)
                step(v.tensor_scalar(en[:], en[:], 1.0, None, ALU.add))
                step(v.reciprocal(aff[:], en[:]))
                step(v.tensor_tensor(biased[:], aff[:], bias_all[:].unsqueeze(1).broadcast_to([P, BT, E]), ALU.add))
                for t in range(BT):
                    ins = v.max(top8[:, t, :], biased[:, t, :])
                step(ins)
                for t in range(BT):
                    ins = v.max_index(top8_at[:, t, :], top8[:, t, :], biased[:, t, :])
                step(ins)
                step(v.tensor_copy(top_at[:].rearrange("p c t -> p t c"), top8_at[:, :, 0:2]))
                step(v.tensor_tensor(hot[:], iota_f[:, 0:E].unsqueeze(1).unsqueeze(1).broadcast_to([P, 2, BT, E]),
                                     over_e(top_at[:]), ALU.is_equal))
                v.tensor_tensor(hot_b[:, 0:BT], hot[:, 0], hot[:, 1], ALU.add).then_inc(hot_done, 1)

            def take_ranks(b, at=5):
                wait_apart(dve, ranks, b + 1)
                v.tensor_tensor(pos[:], bank[:, at, 0:BT * E].rearrange("p (t e) -> p t e", t=BT),
                                list_at[:].unsqueeze(1).broadcast_to([P, BT, E]), ALU.add).then_inc(ranks_read, 1)

            def weigh(b):
                step(v.tensor_tensor(picked[:], hot[:], both_experts(aff[:]), ALU.mult))
                step(v.tensor_reduce(taff[:], picked[:], AX, ALU.add))
                step(v.tensor_tensor(tsum[:], taff[:, 0], taff[:, 1], ALU.add))
                step(v.tensor_scalar(tsum[:], tsum[:], GATE_EPS, None, ALU.add))
                step(v.reciprocal(tsum[:], tsum[:]))
                if not isinstance(b, int) or b > 0:
                    wait_apart(dve, rows_named, 3 * b)
                v.tensor_tensor(weight[:], taff[:], tsum[:].unsqueeze(1).broadcast_to([P, 2, BT]), ALU.mult).then_inc(weights_done, 1)

            def place(b):
                wait_apart(dve, ranks_read, b + 1)
                step(v.tensor_tensor(picked[:], hot[:], both_experts(pos[:]), ALU.mult))
                step(v.tensor_reduce(slot_f[:], picked[:], AX, ALU.add))
                wait_apart(dve, rows_free, b + 1)
                v.tensor_copy(slot_u[:], slot_f[:]).then_inc(slots_done, 1)
                assert n_step[0] == ROUTE_STEPS

            def count_in(b):
                v.tensor_reduce(in_batch[:], hot_b[:, 0:BT].rearrange("p t e -> p e t"), AX, ALU.add).then_inc(sum_step, 1)
                wait_apart(dve, sum_step, b + 1)
                v.tensor_tensor(hot_sum[:], hot_sum[:], in_batch[:], ALU.add).then_inc(sum_done, 1)

            def shared_hidden(b, *halves):
                for half in halves:
                    dve.wait_ge(a_gs, HALVES * b + half + 1)
                    dve.wait_ge(pe_u, HALVES * b + half + 1)
                    v.tensor_tensor(hs[:, half, :], hs[:, half, :], bank[:, 4 + half, :], ALU.mult).then_inc(d_hs, 1)

            def add_shared(b):
                for n in range(2):
                    wait_apart(dve, pe_down, 2 * b + n + 1)
                    r = res[:, bass.ds(BT * b + 2 * n, 2), :].rearrange("p t d -> p (t d)")
                    v.scalar_tensor_tensor(out=r, in0=bank[:, 4 + n, :], scalar=SHARED_RATIO, in1=r,
                                           op0=ALU.mult, op1=ALU.add).then_inc(d_shared, 1)

            def clamped(b, at=5):
                dve.wait_ge(pe_logit, b + 1)
                v.tensor_scalar(logit[:], bank[:, at, 0:BT * E].rearrange("p (t e) -> p t e", t=BT),
                                LEAST_LOGIT, None, ALU.max).then_inc(d_logit, 1)

            def batch(b, first, last):
                need(dve, pe_o, BT * b)
                for n in range(2):
                    dve.wait_ge(a_v, 2 * b + n + 1)
                    sub(v_lo[:, 2 * n:2 * n + 2, :].rearrange("p t d -> p (t d)"), bank[:, n, :],
                        v_hi[:, 2 * n:2 * n + 2, :].rearrange("p t d -> p (t d)")).then_inc(d_v, 1)
                if not first:
                    normalized(b - 1)
                for m in range(KC):
                    dve.wait_ge(a_qT, KC * b + m + 1)
                    sub(qT_lo[:, m, :], bank[:, 2 + m, :], qT_hi[:, m, :]).then_inc(d_qT, 1)
                if not first:
                    transposed(b - 1, a_x2T, d_x2T, x2T_lo, x2T_hi, 4, pe_o, BT * b)
                def row_max(n):
                    i = BT - 1 - n
                    dve.wait_ge(pe_s, BT * b + n + 1)
                    v.reduce_max(smax[:, i:i + 1], bank[:, 6 + n % 2, 0:(i + 1) * P], AX).then_inc(d_max, 1)
                    dve.wait_ge(d_max, BT * b + n + 1)
                    v.tensor_scalar(nbias[:, i:i + 1], smax[:, i:i + 1], -SCALE, None, ALU.mult).then_inc(d_nbias, 1)

                def probsT(n):
                    cols = (BT - n) * P
                    dve.wait_ge(a_pT, BT * b + n + 1)
                    need(dve, pe_o, BT * b + max(n - 1, 0))
                    sub(pT_lo[:, n % 2, 0:cols], bank[:, n % 2, 0:cols], pT_hi[:, n % 2, 0:cols]).then_inc(d_pT, 1)

                def attended(n):
                    i = BT - 1 - n
                    dve.wait_ge(a_exp, BT * b + n + 1)
                    v.reciprocal(rinv[:, i:i + 1], rsum[:, i:i + 1]).then_inc(d_rinv, 1)
                    dve.wait_ge(d_rinv, BT * b + n + 1)
                    dve.wait_ge(pe_o, BT * b + n + 1)
                    r = res_tile(b, i)
                    v.scalar_tensor_tensor(out=r, in0=bank[:, 2 + n % 2, 0:D], scalar=rinv[:, i:i + 1], in1=r,
                                           op0=ALU.mult, op1=ALU.add).then_inc(d_o, 1)

                def attended_stats(n):
                    wait_apart(dve, d_o, BT * b + n + 1)
                    v.bn_stats(stats2[:, BT - 1 - n, :], res_tile(b, BT - 1 - n)).then_inc(ln2_stats, 1)

                row_max(0)
                row_max(1)
                if not first:
                    clamped(b - 1)
                    if not last:
                        normalized_input(b + 1)
                    choose(b - 1)
                    shared_hidden(b - 1, *range(HALVES))
                probsT(0)
                row_max(2)
                if first:
                    normalized_input(b + 1)
                else:
                    weigh(b - 1)
                attended(0)
                probsT(1)
                row_max(3)
                attended_stats(0)
                if not first:
                    take_ranks(b - 1)
                attended(1)
                probsT(2)
                attended_stats(1)
                if not last:
                    transposed(b + 1, a_xT, d_xT, xT_lo, xT_hi, 6, pe_s, BT * (b + 1), [0])
                else:
                    place(b - 1)
                    count_in(b - 1)
                attended(2)
                probsT(3)
                if not last:
                    transposed(b + 1, a_xT, d_xT, xT_lo, xT_hi, 6, pe_s, BT * (b + 1), [1])
                attended_stats(2)
                attended(3)
                attended_stats(3)
                batch_stats(b)
                if not first and not last:
                    place(b - 1)
                    count_in(b - 1)
                    add_shared(b - 1)

            over_batches(dve, batch)
            dve.wait_ge(rows_copied, 2 * (B - 1))
            normalized(B - 1)
            transposed(B - 1, a_x2T, d_x2T, x2T_lo, x2T_hi, 6, pe_o, BT * B)
            add_shared(B - 2)
            clamped(B - 1, 3)
            choose(B - 1)
            weigh(B - 1)
            take_ranks(B - 1, 3)
            place(B - 1)
            count = bank[:, 3, BT * E:(BT + 1) * E]
            v.tensor_tensor(pad_at[:], count, list_at[:], ALU.add).then_inc(pads_done, 1)
            v.tensor_scalar(cnt[:], count, float(P - 1), None, ALU.add).then_inc(ranks_read, 1)
            shared_hidden(B - 1, *range(HALVES))
            for half in range(HALVES):
                dve.wait_ge(a_hs, HALVES * (B - 1) + half + 1)
                sub(hs_lo[:, half, :], hs[:, half, :], hs_hi[:, half, :]).then_inc(hs_split, 1)
            step_base[0], n_step[0] = ROUTE_STEPS * B, 0
            dve.wait_ge(ranks_read, B + 1)
            dve.wait_ge(hs_split, HALVES * B)
            step(v.tensor_copy(cnt_i[:], cnt[:]))
            step(v.tensor_scalar(cnt_i[:], cnt_i[:], P.bit_length() - 1, None, ALU.arith_shift_right))
            step(v.tensor_copy(tiles_f[:], cnt_i[:]))
            step(v.tensor_tensor_scan(ends[:], ones_e[:], tiles_f[:], 0.0, ALU.mult, ALU.add))
            step(v.tensor_scalar(gap[:], tiles_f[:], -1.0, float(LIST_TILES), ALU.mult, ALU.add))
            step(v.tensor_tensor(past[:], ends[0:1, :].unsqueeze(1).broadcast_to([1, EXPERT_TILES, E]),
                                 iota_f[0:1, :].unsqueeze(2).broadcast_to([1, EXPERT_TILES, E]), ALU.is_le))
            step(v.tensor_tensor(skipped[:], past[:], gap[0:1, :].unsqueeze(1).broadcast_to([1, EXPERT_TILES, E]), ALU.mult))
            step(v.tensor_reduce(tile_f[:], skipped[:], AX, ALU.add))
            step(v.tensor_tensor(tile_f[:], tile_f[:], iota_f[0:1, :], ALU.add))
            step(v.tensor_scalar(tile_f[:], tile_f[:], float(P), None, ALU.mult))
            v.tensor_copy(tile_at[:], tile_f[:]).then_inc(tiles_done, 1)
            step(v.tensor_reduce(tile_expert[:], past[:], AX, ALU.add))
            step(v.tensor_scalar(tile_expert[:], tile_expert[:], float(E - 1), None, ALU.min))
            for k in range(IDS):
                ins = v.memset(digit[:, k:k + 1], float(1 << (ID_BITS * (k % (IDS // 2)))))
            step(ins)
            step(v.tensor_tensor(shifted[:], tile_expert[:].rearrange("a (g k) -> a g k", k=IDS),
                                 digit[:].unsqueeze(1).broadcast_to([1, WORDS, IDS]), ALU.mult))
            for n in range(2):
                ins = v.tensor_reduce(half_f[:, n], shifted[:, :, n * IDS // 2:(n + 1) * IDS // 2], AX, ALU.add)
            step(ins)
            step(v.tensor_copy(half_u[:], half_f[:]))
            step(v.tensor_scalar(half_u[:, 1], half_u[:, 1], ID_BITS * IDS // 2, None, ALU.logical_shift_left))
            v.tensor_tensor(word[:], half_u[:, 0], half_u[:, 1], ALU.bitwise_or).then_inc(words_done, 1)
            add_shared(B - 1)
            def tile_lo(q, k):
                J = RING * q + k
                dve.wait_ge(a_t, J + 1)
                sub(gT_lo[:, k % 4, :], bank[:, k % 2, 0:D], gT_hi[:, k % 4, :]).then_inc(d_t, 1)

            def tile_lo_and_gate(q, k):
                tile_lo(q, k)
                need(dve, sc_y[k], 16 * q)
                v.tensor_copy(dest[:, k:k + 1], ring[:, k, D:D + 1].bitcast(U32)).then_inc(d_dest, 1)
                v.tensor_copy(gate[:, k:k + 1], ring[:, k, D + 1:D + 2]).then_inc(d_dest, 1)

            def hidden(q, k):
                J = RING * q + k
                dve.wait_ge(a_silu, J + 1)
                v.tensor_tensor(h[:, k % 2, :], sg[:, k % 2, :], bank[:, 2 + k % 2, I:2 * I], ALU.mult).then_inc(d_h, 1)

            def hidden_lo(q, k):
                J = RING * q + k
                dve.wait_ge(a_hT, J + 1)
                sub(hT_lo[:, k % 2, :], bank[:, 4 + k % 2, 0:P], hT_hi[:, k % 2, :]).then_inc(d_hT, 1)

            pipelined(dve, [(2, tile_lo_and_gate), (0, hidden), (-1, hidden_lo)])

            for n in range(CHUNKS):
                r = res[:, n * CT:(n + 1) * CT, :]
                dve.wait_ge(ld_both[n % 4], 16 * (n // 4 + 1))
                v.tensor_tensor(r, r, both[:, n % 4, :, 0, :], ALU.add).then_inc(f_part, 1)
                dve.wait_ge(f_part, n + 1)
                v.tensor_tensor(r, r, both[:, n % 4, :, 1, :], ALU.add).then_inc(f_done, 1)

        @block.tensor
        def _(pe):
            def transpose_rows(src, c, to, made):
                for t in range(BT):
                    ins = pe.transpose(bank[:, to, t * P:(t + 1) * P], src[:, t, c * P:(c + 1) * P], ident[:])
                ins.then_inc(made, 1)

            pe.wait_ge(ld_wqk, 32)
            pe.wait_ge(consts, 1)
            for n in range(2):
                for c in range(KC):
                    for r in range(KC):
                        ins = pe.transpose(bank[:, n, c * D + r * P:c * D + (r + 1) * P],
                                           wqk_raw[:, n, r, c * P:(c + 1) * P], ident[:])
                ins.then_inc(wT_done, 1)
            pe.wait_ge(ln1_done, BT)
            for c in range(KC):
                transpose_rows(xn, c, 6 + c, pe_xT)
            pe.wait_ge(ld_cen, 16)
            for c in range(KC):
                ins = pe.transpose(bank[:, 3, c * E:(c + 1) * E], cen_raw[:, c * P:(c + 1) * P], ident[0:E, 0:E])
            ins.then_inc(cenT, 1)
            pe.wait_ge(wT_copied, 2)
            for r in range(KC):
                for c in range(KC):
                    ins = pe.matmul(bank[:, 2, r * D:(r + 1) * D], wqkT[:, 0, c, r * P:(r + 1) * P], wqkT[:, 1, c, :],
                                    start=(c == 0), stop=(c == KC - 1))
            ins.then_inc(a_done, 1)
            pe.wait_ge(wv_done, 2)

            def logits_T(b, to=4):
                pe.wait_ge(d_x2T, KC * (b + 1))
                for c in range(KC):
                    ins = split3(pe, bank[0:E, to, :], cen_hi[:, c, :], cen_lo[:, c, :], x2T_hi[:, c, :], x2T_lo[:, c, :],
                                 c == 0, c == KC - 1)
                ins.then_inc(pe_logit_T, 1)

            def logits(b, to=5):
                wait_apart(pe, a_logit_T, b + 1)
                for t in range(BT):
                    ins = pe.transpose(bank[:, to, t * E:(t + 1) * E], logit_T[:, t * P:(t + 1) * P], ident[0:E, 0:E])
                ins.then_inc(pe_logit, 1)

            def shared_in(b, part, to, made, halves=range(HALVES), chunks=range(KC)):
                for half in halves:
                    for c in chunks:
                        at = slice((2 * c + part) * I, (2 * c + part + 1) * I)
                        ins = split3(pe, bank[:, to + half, :], w_hi[:, E + half, at], w_lo[:, E + half, at],
                                     x2T_hi[:, c, :], x2T_lo[:, c, :], c == 0, c == KC - 1)
                    if chunks[-1] == KC - 1:
                        ins.then_inc(made, 1)

            def shared_down(b, tiles=range(BT)):
                pe.wait_ge(hs_split, HALVES * (b + 1))
                at = slice(KC * 2 * I, WE)
                for t in tiles:
                    if t == 2:
                        pe.wait_ge(ranks_read, b + 1)
                    for half in range(HALVES):
                        own = slice(t * P, (t + 1) * P)
                        ins = split3(pe, bank[:, 4 + t // 2, t % 2 * D:(t % 2 + 1) * D], hs_hi[:, half, own], hs_lo[:, half, own],
                                     w_hi[:, E + half, at], w_lo[:, E + half, at], half == 0, half == HALVES - 1)
                    if t % 2 == 1:
                        ins.then_inc(pe_down, 1)

            def rank(b, ranked, of_bank):
                pe.wait_ge(hot_done, b + 1)
                pe.wait_ge(*of_bank)
                ranked = ranked[:, 0:(BT + 1) * E]
                pe.matmul(ranked, before_b[:], hot_b[:].rearrange("p t e -> p (t e)"), start=True, stop=False)
                for t in range(BT):
                    pe.matmul(ranked[:, (t + 1) * E:].rearrange("p (t e) -> p t e", e=E), ones_b[:],
                              hot_b[:, t:t + 1, :].broadcast_to([P, BT - t, E]), start=False, stop=False)
                pe.matmul(ranked.rearrange("p (t e) -> p t e", e=E), ones_b[:],
                          hot_sum[:].unsqueeze(1).broadcast_to([P, BT + 1, E]), start=False, stop=True).then_inc(ranks, 1)

            def batch(b, first, last):
                pe.wait_ge(d_xT, KC * (b + 1))
                need(pe, d_pT, BT * b)
                for n in range(2):
                    for t in (2 * n, 2 * n + 1):
                        for c in range(KC):
                            at = slice(t * P, (t + 1) * P)
                            ins = split3(pe, bank[:, n, t % 2 * D:(t % 2 + 1) * D], xT_hi[:, c, at], xT_lo[:, c, at],
                                         wv_hi[:, c, :], wv_lo[:, c, :], c == 0, c == KC - 1)
                    ins.then_inc(pe_v, 1)
                if first:
                    pe.wait_ge(a_lo_done, 1)
                    pe.wait_ge(cen_done, 1)
                need(pe, d_o, BT * b)
                for m in range(KC):
                    for c in range(KC):
                        at = slice(m * P, (m + 1) * P)
                        ins = split3(pe, bank[:, 2 + m, :], a_hi[:, c, at], a_lo[:, c, at], xT_hi[:, c, :], xT_lo[:, c, :],
                                     c == 0, c == KC - 1)
                    ins.then_inc(pe_qT, 1)
                if not first:
                    pe.wait_ge(ln2_done, BT * b)
                    for c in range(KC):
                        transpose_rows(x2, c, 4 + c, pe_x2T)

                def scores(n):
                    i = BT - 1 - n
                    need(pe, a_exp, BT * b + max(n - 1, 0))
                    s = bank[:, 6 + n % 2, :]
                    cols = max((i + 1) * P, 2 * P)
                    at = slice(i * P, (i + 1) * P)
                    for m in range(KC):
                        split3(pe, s[:, 0:cols], qT_hi[:, m, at], qT_lo[:, m, at], xT_hi[:, m, 0:cols],
                               xT_lo[:, m, 0:cols], m == 0, False)
                    pe.matmul(s[:, at], ident_b[:], mask_b[:], start=False, stop=True).then_inc(pe_s, 1)

                def probsT(n):
                    pe.wait_ge(a_exp, BT * b + n + 1)
                    if n > 1:
                        pe.wait_ge(d_pT, BT * b + n - 1)
                    for kb in range(BT - n):
                        at = slice(kb * P, (kb + 1) * P)
                        ins = pe.transpose(bank[:, n % 2, at], probs[:, n % 2, at], ident[:])
                    ins.then_inc(pe_pT, 1)

                def attend(n):
                    pe.wait_ge(d_pT, BT * b + n + 1)
                    if n > 1:
                        pe.wait_ge(d_o, BT * b + n - 1)
                    for kb in range(BT - n):
                        at = slice(kb * P, (kb + 1) * P)
                        ins = split3(pe, bank[:, 2 + n % 2, 0:D], pT_hi[:, n % 2, at], pT_lo[:, n % 2, at],
                                     v_hi[:, kb, :], v_lo[:, kb, :], kb == 0, kb == BT - 1 - n)
                    ins.then_inc(pe_o, 1)

                pe.wait_ge(d_qT, KC * (b + 1))
                scores(0)
                if not first:
                    logits_T(b - 1)
                scores(1)
                if not first:
                    logits(b - 1)
                pe.wait_ge(d_v, 2 * (b + 1))
                if not first:
                    shared_in(b - 1, 0, 0, pe_g)
                    pe.wait_ge(d_logit, b)
                    shared_in(b - 1, 1, 4, pe_u)
                    pe.wait_ge(a_gs, HALVES * b)
                probsT(0)
                scores(2)
                attend(0)
                probsT(1)
                scores(3)
                if not first:
                    rank(b - 1, bank[:, 5], (d_hs, HALVES * b))
                attend(1)
                probsT(2)
                if not last:
                    pe.wait_ge(ln1_done, BT * (b + 2))
                    transpose_rows(xn, 0, 6, pe_xT)
                attend(2)
                probsT(3)
                if not last:
                    transpose_rows(xn, 1, 7, pe_xT)
                attend(3)
                if not first and not last:
                    shared_down(b - 1)

            over_batches(pe, batch)
            shared_down(B - 2, [0, 1, 2])
            pe.wait_ge(ln2_done, BT * B)
            for c in range(KC):
                transpose_rows(x2, c, 6 + c, pe_x2T)
            shared_down(B - 2, [3])
            pe.wait_ge(d_o, BT * B)
            logits_T(B - 1, 2)
            pe.wait_ge(d_pT, BT * B)
            shared_in(B - 1, 0, 0, pe_g, [0], [0])
            logits(B - 1, 3)
            shared_in(B - 1, 0, 0, pe_g, [0], [1])
            shared_in(B - 1, 0, 0, pe_g, [1])
            pe.wait_ge(d_shared, 2 * (B - 1))
            shared_in(B - 1, 1, 4, pe_u, [0])
            rank(B - 1, bank[:, 3], (d_logit, B))
            shared_in(B - 1, 1, 4, pe_u, [1])
            shared_down(B - 1)
            def transpose_tile(q, k):
                J = RING * q + k
                pe.wait_ge(ld_t[k], 16 * (q + 1))
                for c in range(KC):
                    ins = pe.transpose(bank[:, k % 2, c * P:(c + 1) * P], ring[:, k, c * P:(c + 1) * P], ident[:])
                ins.then_inc(pe_t, 1)

            def weights_of(e, at):
                if isinstance(e, int):
                    return w_hi[:, e, at], w_lo[:, e, at]
                return w_hi[:, bass.ds(e, 1), at], w_lo[:, bass.ds(e, 1), at]

            def await_tile(q, k):
                pe.wait_ge(d_t, RING * q + k + 1)

            def await_hidden(q, k):
                pe.wait_ge(d_hT, RING * q + k + 1)

            def gate_up(q, k, e, beside):
                for c in range(KC):
                    at = slice(c * P, (c + 1) * P)
                    rhi, rlo = weights_of(e, slice(c * 2 * I, (c + 1) * 2 * I))
                    ins = split3(pe, bank[:, 2 + k % 2, 0:2 * I], gT_hi[:, k % 4, at], gT_lo[:, k % 4, at], rhi, rlo,
                                 c == 0, c == KC - 1)
                    if c == 0:
                        beside()
                ins.then_inc(pe_gu, 1)

            def hidden_T(q, k):
                J = RING * q + k
                pe.wait_ge(d_h, J + 1)
                pe.transpose(bank[:, 4 + k % 2, 0:P], h[:, k % 2, :], ident[:]).then_inc(pe_hT, 1)

            def down(q, k, e):
                rhi, rlo = weights_of(e, slice(KC * 2 * I, WE))
                split3(pe, bank[:, 6 + k % 2, 0:D], hT_hi[:, k % 2, :], hT_lo[:, k % 2, :], rhi, rlo, True, True)\
                    .then_inc(pe_y, 1)

            pe.wait_ge(w_lo_done, E + HALVES)
            pe.wait_ge(a_gs, HALVES * B)
            pe.wait_ge(d_shared, 2 * B)
            pe.wait_ge(words_done, 1)
            words = [pe.alloc_register(f"word{n}") for n in range(GROUPS + 1)]
            for n in range(GROUPS):
                pe.reg_load(words[n + 1], word[0:1, n:n + 1])
            experts, packed = {}, {}

            def take_expert(j):
                experts[j] = pe.snap((packed[j >= 0] >> (ID_BITS * (j % IDS))) & (E - 1), min_val=0, max_val=E - 1)

            def begin_group(q):
                packed[True] = pe.snap(words[1])
                if not isinstance(q, int) or q > 0:
                    packed[False] = pe.snap(words[0])
                    take_expert(-2)
                    take_expert(-1)
                take_expert(0)

            def routed_gate_up(q, k):
                def beside():
                    if k + 1 < RING:
                        take_expert(k + 1)
                    elif q is not GROUPS - 1:
                        for n in range(GROUPS):
                            pe.reg_mov(words[n], words[n + 1])
                gate_up(q, k, experts[k], beside)

            def routed_down(q, k):
                down(q, k, experts[position[0]])

            pipelined(pe, [(0, await_tile), (2, transpose_tile), (0, routed_gate_up), (-2, await_hidden), (-1, hidden_T),
                           (-2, routed_down)], begin_group)


_INS = ['L0_attn_x', 'L0_attn_Wq', 'L0_attn_Wk', 'L0_attn_Wv', 'L0_ffn_centroids', 'L0_ffn_gate_bias', 'L0_ffn_wg_s',
        'L0_ffn_wu_s', 'L0_ffn_wd_s', 'L0_ffn_wg', 'L0_ffn_wu', 'L0_ffn_wd']
_OUTS = [((4, 512, 256), 'float32')]


def kernel(**inputs):
    import numpy as _np
    import concourse.bacc as _bacc
    from concourse import mybir as _mybir
    from concourse.bass_utils import run_bass_kernel_spmd as _run

    nc = _bacc.Bacc("TRN2", target_bir_lowering=False, num_devices=1)
    arrays, args = {}, []
    for name in _INS:
        a = _np.ascontiguousarray(inputs[name])
        arrays[f"in_{name}_dram"] = a
        args.append(nc.dram_tensor(f"in_{name}_dram", a.shape, _mybir.dt.from_np(a.dtype), kind="ExternalInput").ap())
    for i, (shape, dtype) in enumerate(_OUTS):
        dt = _mybir.dt.from_np(_np.dtype(dtype))
        args.append(nc.dram_tensor(f"out_{i}_dram", shape, dt, kind="ExternalOutput").ap())
    block_causal_attention_and_moe(nc, *args)
    r = _run(nc, [arrays], core_ids=[0])
    got = tuple(r.results[0][f"out_{i}_dram"] for i in range(len(_OUTS)))
    return got[0]
```
